# Optimizing a Trainium2 kernel written in Bass

```python
import numpy as np
import jax
import jax.numpy as jnp

def _softmax(x, axis=-1):
    return jax.nn.softmax(x, axis=axis)

def _gelu(x):
    return jax.nn.gelu(x, approximate=True)

def _silu(x):
    return jax.nn.silu(x)

def _sigmoid(x):
    return jax.nn.sigmoid(x)

def _layernorm(x, axis=-1, eps=1e-05):
    m = jnp.mean(x, axis=axis, keepdims=True)
    v = jnp.var(x, axis=axis, keepdims=True)
    return (x - m) / jnp.sqrt(v + eps)

def _scatter_add(tgt, idx, src, axis=0):
    return tgt.at[idx].add(src)

def _segment_sum(src, seg, n):
    return jax.ops.segment_sum(src, seg, n)
kernel_name = 'mk_cond_seq_d2_seqx_r4_5d80af'

def setup_inputs(seed: int=0):
    np.random.seed(seed)
    _w = jnp.asarray

    def _rec_inputs():
        import jax
        import jax.numpy as jnp
        _rk = jax.random.key(seed)
        x = -0.0003482 + 1 * jax.random.normal(jax.random.fold_in(_rk, 1), (4, 512, 288), jnp.float32)
        _lenS = 512 - jax.random.randint(jax.random.fold_in(_rk, 7), (4,), 0, max(1, 512 // 4) + 1, jnp.int32)
        _lenS2 = 512 - jax.random.randint(jax.random.fold_in(_rk, 8), (4,), 0, max(1, 512 // 4) + 1, jnp.int32)
        cond_1152 = 0.00257642 + 1.0011 * jax.random.normal(jax.random.fold_in(_rk, 11), (4, 288), jnp.float32)
        return (x, cond_1152)
    x, cond_1152 = _rec_inputs()

    def _L0_cond_setup():
        import jax, jax.numpy as jnp
        import numpy as np
        H = 288
        NH = 16
        HD = H // NH
        MLP = int(H * 4.0)
        EPS = 1e-06

        def _ln(z, scale=None):
            m = jnp.mean(z, axis=-1, keepdims=True)
            v = jnp.mean(jnp.square(z - m), axis=-1, keepdims=True)
            y = (z - m) * jax.lax.rsqrt(v + EPS)
            if scale is not None:
                y = y * scale
            return y
        key = jax.random.key(seed)
        ks = jax.random.split(key, 16)
        B, N = (16, 256)
        x = jax.random.normal(ks[0], (B, N, H), dtype=jnp.float32)
        c = jax.random.normal(ks[1], (B, H), dtype=jnp.float32)

        def xav(k, fan_in, fan_out):
            lim = np.sqrt(6.0 / (fan_in + fan_out))
            return jax.random.uniform(k, (fan_in, fan_out), jnp.float32, -lim, lim)
        w_mod = 0.02 * jax.random.normal(ks[2], (H, 6 * H), dtype=jnp.float32)
        b_mod = 0.02 * jax.random.normal(ks[3], (6 * H,), dtype=jnp.float32)
        w_qkv = xav(ks[4], H, 3 * H)
        b_qkv = jnp.zeros((3 * H,), jnp.float32)
        g_q = jnp.ones((HD,), jnp.float32)
        g_k = jnp.ones((HD,), jnp.float32)
        w_proj = xav(ks[5], H, H)
        b_proj = jnp.zeros((H,), jnp.float32)
        w1 = xav(ks[6], H, MLP)
        b1 = jnp.zeros((MLP,), jnp.float32)
        w2 = xav(ks[7], MLP, H)
        b2 = jnp.zeros((H,), jnp.float32)
        return dict(x=x, c=c, w_mod=w_mod, b_mod=b_mod, w_qkv=w_qkv, b_qkv=b_qkv, g_q=g_q, g_k=g_k, w_proj=w_proj, b_proj=b_proj, w1=w1, b1=b1, w2=w2, b2=b2)
    _L0_cond_all = _L0_cond_setup()
    _L0_cond_in = {k: v for k, v in _L0_cond_all.items() if k in ('w_mod', 'b_mod', 'w_qkv', 'b_qkv', 'g_q', 'g_k', 'w_proj', 'b_proj', 'w1', 'b1', 'w2', 'b2')}
    del _L0_cond_all

    def _L1_cond_setup():
        import jax, jax.numpy as jnp
        import numpy as np
        NUM_HEADS = 16
        NUM_EXPERTS = 4
        TOP_K = 2
        LN_EPS = 1e-06

        def _ln(h):
            mu = jnp.mean(h, axis=-1, keepdims=True)
            var = jnp.var(h, axis=-1, keepdims=True)
            return (h - mu) * jax.lax.rsqrt(var + LN_EPS)

        def _modulate(h, shift, scale):
            return h * (1.0 + scale[:, None, :]) + shift[:, None, :]
        key = jax.random.key(seed)
        ks = jax.random.split(key, 12)
        B, N, C = (8, 256, 288)
        H = 4 * C
        E = NUM_EXPERTS
        s = 0.02
        return {'x': jax.random.normal(ks[0], (B, N, C), jnp.float32), 'c': jax.random.normal(ks[1], (B, C), jnp.float32), 'w_adaln': jax.random.normal(ks[2], (C, 6 * C), jnp.float32) * s, 'b_adaln': jnp.zeros((6 * C,), jnp.float32), 'w_qkv': jax.random.normal(ks[3], (C, 3 * C), jnp.float32) * s, 'b_qkv': jnp.zeros((3 * C,), jnp.float32), 'w_proj': jax.random.normal(ks[4], (C, C), jnp.float32) * s, 'b_proj': jnp.zeros((C,), jnp.float32), 'w_gate': jax.random.normal(ks[5], (C, E), jnp.float32) * s, 'w1': jax.random.normal(ks[6], (E, C, H), jnp.float32) * s, 'b1': jnp.zeros((E, H), jnp.float32), 'w2': jax.random.normal(ks[7], (E, H, C), jnp.float32) * s, 'b2': jnp.zeros((E, C), jnp.float32)}
    _L1_cond_all = _L1_cond_setup()
    _L1_cond_in = {k: v for k, v in _L1_cond_all.items() if k in ('w_adaln', 'b_adaln', 'w_qkv', 'b_qkv', 'w_proj', 'b_proj', 'w_gate', 'w1', 'b1', 'w2', 'b2')}
    del _L1_cond_all
    return {'x': x, 'cond_1152': cond_1152, 'L0_cond_w_mod': _L0_cond_in['w_mod'], 'L0_cond_b_mod': _L0_cond_in['b_mod'], 'L0_cond_w_qkv': _L0_cond_in['w_qkv'], 'L0_cond_b_qkv': _L0_cond_in['b_qkv'], 'L0_cond_g_q': _L0_cond_in['g_q'], 'L0_cond_g_k': _L0_cond_in['g_k'], 'L0_cond_w_proj': _L0_cond_in['w_proj'], 'L0_cond_b_proj': _L0_cond_in['b_proj'], 'L0_cond_w1': _L0_cond_in['w1'], 'L0_cond_b1': _L0_cond_in['b1'], 'L0_cond_w2': _L0_cond_in['w2'], 'L0_cond_b2': _L0_cond_in['b2'], 'L1_cond_w_adaln': _L1_cond_in['w_adaln'], 'L1_cond_b_adaln': _L1_cond_in['b_adaln'], 'L1_cond_w_qkv': _L1_cond_in['w_qkv'], 'L1_cond_b_qkv': _L1_cond_in['b_qkv'], 'L1_cond_w_proj': _L1_cond_in['w_proj'], 'L1_cond_b_proj': _L1_cond_in['b_proj'], 'L1_cond_w_gate': _L1_cond_in['w_gate'], 'L1_cond_w1': _L1_cond_in['w1'], 'L1_cond_b1': _L1_cond_in['b1'], 'L1_cond_w2': _L1_cond_in['w2'], 'L1_cond_b2': _L1_cond_in['b2']}

def reference(x, cond_1152, L0_cond_w_mod, L0_cond_b_mod, L0_cond_w_qkv, L0_cond_b_qkv, L0_cond_g_q, L0_cond_g_k, L0_cond_w_proj, L0_cond_b_proj, L0_cond_w1, L0_cond_b1, L0_cond_w2, L0_cond_b2, L1_cond_w_adaln, L1_cond_b_adaln, L1_cond_w_qkv, L1_cond_b_qkv, L1_cond_w_proj, L1_cond_b_proj, L1_cond_w_gate, L1_cond_w1, L1_cond_b1, L1_cond_w2, L1_cond_b2):
    import jax
    import jax.numpy as jnp

    def _L0_cond_ref(x, c, w_mod, b_mod, w_qkv, b_qkv, g_q, g_k, w_proj, b_proj, w1, b1, w2, b2):
        import jax, jax.numpy as jnp
        import numpy as np
        H = 288
        NH = 16
        HD = H // NH
        MLP = int(H * 4.0)
        EPS = 1e-06

        def _ln(z, scale=None):
            m = jnp.mean(z, axis=-1, keepdims=True)
            v = jnp.mean(jnp.square(z - m), axis=-1, keepdims=True)
            y = (z - m) * jax.lax.rsqrt(v + EPS)
            if scale is not None:
                y = y * scale
            return y
        B, N, _ = x.shape
        mod = jax.nn.swish(c) @ w_mod + b_mod
        sh_msa, sc_msa, g_msa, sh_mlp, sc_mlp, g_mlp = jnp.split(mod, 6, axis=1)
        xn = _ln(x) * (1 + sc_msa[:, None, :]) + sh_msa[:, None, :]
        qkv = xn @ w_qkv + b_qkv
        qkv = qkv.reshape(B, N, 3, NH, HD).transpose(2, 0, 3, 1, 4)
        q, k, v = (qkv[0], qkv[1], qkv[2])
        q = _ln(q, g_q)
        k = _ln(k, g_k)
        attn = jax.nn.softmax(jnp.einsum('bhqd,bhkd->bhqk', q, k) * HD ** (-0.5), axis=-1)
        o = jnp.einsum('bhqk,bhkd->bhqd', attn, v)
        o = o.transpose(0, 2, 1, 3).reshape(B, N, H) @ w_proj + b_proj
        x = x + g_msa[:, None, :] * o
        xn2 = _ln(x) * (1 + sc_mlp[:, None, :]) + sh_mlp[:, None, :]
        h = jax.nn.gelu(xn2 @ w1 + b1, approximate=True)
        x = x + g_mlp[:, None, :] * (h @ w2 + b2)
        return x

    def _L1_cond_ref(x, c, w_adaln, b_adaln, w_qkv, b_qkv, w_proj, b_proj, w_gate, w1, b1, w2, b2):
        import jax, jax.numpy as jnp
        import numpy as np
        NUM_HEADS = 16
        NUM_EXPERTS = 4
        TOP_K = 2
        LN_EPS = 1e-06

        def _ln(h):
            mu = jnp.mean(h, axis=-1, keepdims=True)
            var = jnp.var(h, axis=-1, keepdims=True)
            return (h - mu) * jax.lax.rsqrt(var + LN_EPS)

        def _modulate(h, shift, scale):
            return h * (1.0 + scale[:, None, :]) + shift[:, None, :]
        B, N, C = x.shape
        nh = NUM_HEADS
        hd = C // nh
        mod = jax.nn.silu(c) @ w_adaln + b_adaln
        sh_msa, sc_msa, g_msa, sh_mlp, sc_mlp, g_mlp = jnp.split(mod, 6, axis=-1)
        h = _modulate(_ln(x), sh_msa, sc_msa)
        qkv = (h @ w_qkv + b_qkv).reshape(B, N, 3, nh, hd).transpose(2, 0, 3, 1, 4)
        q, k, v = (qkv[0], qkv[1], qkv[2])
        attn = jax.nn.softmax(jnp.einsum('bhqd,bhkd->bhqk', q, k) * hd ** (-0.5), axis=-1)
        o = jnp.einsum('bhqk,bhkd->bhqd', attn, v).transpose(0, 2, 1, 3).reshape(B, N, C)
        o = o @ w_proj + b_proj
        x = x + g_msa[:, None, :] * o
        xn = _modulate(_ln(x), sh_mlp, sc_mlp)
        xf = xn.reshape(-1, C)
        gate_logits = xf @ w_gate
        topk_logits, topk_idx = jax.lax.top_k(gate_logits, TOP_K)
        gates = jax.nn.softmax(topk_logits, axis=-1)
        cw = jnp.sum(jax.nn.one_hot(topk_idx, NUM_EXPERTS, dtype=xf.dtype) * gates[..., None], axis=1)
        hmid = jax.nn.gelu(jnp.einsum('tc,ech->eth', xf, w1) + b1[:, None, :], approximate=True)
        eo = jnp.einsum('eth,ehc->etc', hmid, w2) + b2[:, None, :]
        moe = jnp.einsum('te,etc->tc', cw, eo).reshape(B, N, C)
        return x + g_mlp[:, None, :] * moe
    x = _L0_cond_ref(x, cond_1152, L0_cond_w_mod, L0_cond_b_mod, L0_cond_w_qkv, L0_cond_b_qkv, L0_cond_g_q, L0_cond_g_k, L0_cond_w_proj, L0_cond_b_proj, L0_cond_w1, L0_cond_b1, L0_cond_w2, L0_cond_b2)
    x = _L1_cond_ref(x, cond_1152, L1_cond_w_adaln, L1_cond_b_adaln, L1_cond_w_qkv, L1_cond_b_qkv, L1_cond_w_proj, L1_cond_b_proj, L1_cond_w_gate, L1_cond_w1, L1_cond_b1, L1_cond_w2, L1_cond_b2)
    return x

_drawn_inputs = setup_inputs


def setup_inputs(seed=0):
    import zlib

    import numpy as np

    out = dict(_drawn_inputs(seed))
    spreads = {'L0_cond_b_qkv': (0.0, 0.388),
     'L0_cond_g_q': (1.0, 0.6),
     'L0_cond_g_k': (1.0, 0.6),
     'L0_cond_b_proj': (0.0, 0.401),
     'L0_cond_b1': (0.0, 0.516),
     'L0_cond_b2': (0.0, 0.423),
     'L1_cond_b_adaln': (0.0, 0.445),
     'L1_cond_b_qkv': (0.0, 0.8),
     'L1_cond_b_proj': (0.0, 0.389),
     'L1_cond_b1': (0.0, 0.8),
     'L1_cond_b2': (0.0, 0.534)}
    factors = {'L0_cond_b_mod': 5.084,
     'L1_cond_w_qkv': 8.0,
     'L1_cond_w_proj': 5.99,
     'L1_cond_w_gate': 2.979,
     'L1_cond_w1': 2.854}
    for name, (base, spread) in spreads.items():
        noise = np.random.default_rng([zlib.crc32(name.encode()), seed]).standard_normal(out[name].shape)
        drawn = base * np.exp(spread * noise) if base else spread * noise
        out[name] = jnp.asarray(drawn.astype(out[name].dtype))
    for name, factor in factors.items():
        out[name] = (out[name] * factor).astype(out[name].dtype)
    return out
```

```python
from contextlib import ExitStack

import concourse.bass as bass
from concourse import mybir

F32 = mybir.dt.float32
F32R = mybir.dt.float32r
ALU = mybir.AluOpType
ACT = mybir.ActivationFunctionType
AX = mybir.AxisListType.X

P = 128
B = 4
NB = 512
TB = NB // P
T = B * TB
C = 288
CR = C - 2 * P
NH = 16
HD = C // NH
HG = 4
NG = NH // HG
GC = HG * HD
HID = 4 * C
NHC = HID // P
QKW = 2 * C
HALF = 3 * C // 2
EPS = 1e-6
KS_ROWS = 96
M_ROW = 3 * HD


def f(ap):
    return ap.bitcast(F32)


PAIRS = [(0, 0), (1, 1), (0, 2), (1, 3), (2, 0), (3, 1), (4, 4)]


def rows_of(plane):
    return 96 if plane == 4 else P


class BankUses:

    def __init__(self, before, loop):
        self.before, self.loop = before, loop
        self.n_before = [sum(k == bank for _, k in before) for bank in (0, 1)]
        self.n_loop = [sum(k == bank for _, k in loop) for bank in (0, 1)]

    def bank(self, use):
        return dict(self.loop)[use]

    def count(self, use, b=None):
        uses = self.before if b is None else self.loop
        bank = dict(uses)[use]
        at = [u for u, k in uses if k == bank].index(use) + 1
        return at if b is None else b * self.n_loop[bank] + (self.n_before[bank] + at)


LOOP = [("xA", 0), ("xB", 1), ("xC", 0),
        ("max0", 1), ("qkv0a", 0), ("qkv0b", 1), ("qkv1a", 0), ("qkv1b", 1), ("o0", 0),
        ("max1", 1), ("qkv2a", 0), ("qkv2b", 1), ("qkv3a", 0), ("qkv3b", 1), ("o1", 0),
        ("q0", 0), ("k0", 1),
        ("max2", 0), ("q1", 1), ("k1", 0), ("q2", 1), ("k2", 0), ("q3", 1), ("k3", 0), ("o2", 1),
        ("max3", 0), ("o3", 1), ("oA", 0), ("oB", 1), ("oC", 0),
        ("proj0", 1), ("proj1", 0), ("proj2", 1), ("proj3", 0)]
BANK_OF = dict(LOOP)
BEFORE = [(use, BANK_OF[use]) for use in ["xA", "xB", "xC"]
          + [f"qkv{t}{h}" for t in range(TB) for h in "ab"]
          + [f"{s}{g}" for g in range(NG) for s in "qk"] + ["max3"]]
USES = BankUses(BEFORE, LOOP)
SKIPPED = {"xA", "xB", "xC", "max3"} | {f"qkv{t}{h}" for t in range(TB) for h in "ab"} \
    | {f"{s}{g}" for g in range(NG) for s in "qk"}
LAST = [(u, k) for u, k in LOOP if u not in SKIPPED]


def count(use, b, last=False):
    if not last:
        return USES.count(use, b)
    bank = dict(LAST)[use]
    at = [u for u, k in LAST if k == bank].index(use) + 1
    return USES.n_before[bank] + (B - 1) * USES.n_loop[bank] + at


def split_weights(dve, hi_done, n0, stack, raw, raw_rest):
    dve.tensor_copy(stack[:, 0:2, :], raw)
    dve.tensor_copy(stack[0:96, 4, :], raw_rest).then_inc(hi_done, 1)
    dve.wait_ge(hi_done, n0 + 1)
    dve.tensor_tensor(stack[:, 2:4, :], raw, f(stack[:, 0:2, :]), ALU.subtract)
    dve.tensor_tensor(stack[64:96, 4, :], raw_rest[64:96, :], f(stack[64:96, 4, :]),
                      ALU.subtract).then_inc(hi_done, 1)


def setup(nc, sem, sb, pb, L, S, first):
    l = L["l"]
    E = L["E"]
    ctx = ExitStack()
    with ctx:
        wm = sb(ctx, f"wm{l}", [P, 2, 6 * C], F32)
        wm_rest = sb(ctx, f"wm_rest{l}", [CR + 1, 6 * C], F32)
        raw_qkv = sb(ctx, f"raw_qkv{l}", [P, 2, 3 * C], F32)
        raw_qkv_rest = sb(ctx, f"raw_qkv_rest{l}", [96, 3 * C], F32)
        raw_proj = sb(ctx, f"raw_proj{l}", [P, 2, C], F32)
        raw_proj_rest = sb(ctx, f"raw_proj_rest{l}", [96, C], F32)
        raw_gate = sb(ctx, f"raw_gate{l}", [P, 2, 4], F32)
        raw_gate_rest = sb(ctx, f"raw_gate_rest{l}", [96, 4], F32)
        cond = sb(ctx, f"cond{l}", [B, C], F32)
        cond_silu = sb(ctx, f"cond_silu{l}", [B, C], F32)
        mod = sb(ctx, f"mod{l}", [B, 6 * C], F32)
        pick = sb(ctx, f"pick{l}", [B, B, P], F32)
        b1_rows = sb(ctx, f"b1_rows{l}", [E * NHC, P], F32)
        ps_mod = pb(ctx, f"ps_mod{l}", [P, 4, 512], F32)
        ps_small = pb(ctx, f"ps_small{l}", [P, 2, 512], F32)
        ps_gate = pb(ctx, f"ps_gate{l}", [P, 2, 512], F32)

        cond_in = sem(f"cond_in{l}")
        mod_in = sem(f"mod_in{l}")
        attn_in = sem(f"attn_in{l}")
        rows_in = sem(f"rows_in{l}")
        bcast_in = sem(f"bcast_in{l}")
        ident_step = sem(f"ident_step{l}")
        silu_done = sem(f"silu_done{l}")
        ct_ones = sem(f"ct_ones{l}")
        ct_ps = sem(f"ct_ps{l}")
        ct_done = sem(f"ct_done{l}")
        mod_ps = sem(f"mod_ps{l}")
        mod_done = sem(f"mod_done{l}")
        modt_ps = sem(f"modt_ps{l}")
        pick_done = sem(f"pick_done{l}")
        gate_ps = sem(f"gate_ps{l}")
        gate_done = sem(f"gate_done{l}")
        split_step = sem(f"split_step{l}")

        block = ctx.enter_context(nc.Block())

        @block.sync
        def _(sp):
            if l == 0:
                sp.dma_start(cond[:, :], L["cond"]).then_inc(cond_in, 16)
            sp.dma_start(wm[:, :, :], L["w_mod"][0:2 * P, :].rearrange("(k p) n -> p k n", p=P)
                         ).then_inc(mod_in, 16)
            sp.dma_start(wm_rest[0:CR, :], L["w_mod"][2 * P:C, :]).then_inc(mod_in, 16)
            sp.dma_start(wm_rest[CR:CR + 1, :], L["b_mod"].rearrange("(a n) -> a n", a=1)
                         ).then_inc(mod_in, 16)
            for raw, rest, w in ((raw_qkv, raw_qkv_rest, L["w_qkv"]),
                                 (raw_proj, raw_proj_rest, L["w_proj"])):
                sp.dma_start(raw[:, :, :], w[0:2 * P, :].rearrange("(k p) n -> p k n", p=P)
                             ).then_inc(attn_in, 16)
                for r in range(3):
                    sp.dma_start(rest[CR * r:CR * r + CR, :], w[2 * P:C, :]).then_inc(attn_in, 16)
            if E > 1:
                sp.dma_start(raw_gate[:, :, :],
                             L["w_gate"][0:2 * P, :].rearrange("(k p) n -> p k n", p=P)
                             ).then_inc(attn_in, 16)
                for r in range(3):
                    sp.dma_start(raw_gate_rest[CR * r:CR * r + CR, :], L["w_gate"][2 * P:C, :]
                                 ).then_inc(attn_in, 16)
            sp.dma_start(b1_rows[:, :], L["b1"].rearrange("e (k p) -> (e k) p", p=P)
                         ).then_inc(rows_in, 16)
            n = 0
            for dst, src in ((S["bqkv"][:, :], L["b_qkv"]), (S["bproj"][:, :], L["b_proj"])):
                sp.dma_start(dst, src.partition_broadcast(P)).then_inc(bcast_in, 16)
                n += 16
            for e in range(E):
                sp.dma_start(S["b2"][:, e, :], L["b2"][e, :].partition_broadcast(P)
                             ).then_inc(bcast_in, 16)
                n += 16
            if l == 0:
                for i, g in enumerate((L["g_q"], L["g_k"])):
                    sp.dma_start(S["gain"][:, i, :], g.partition_broadcast(P)).then_inc(bcast_in, 16)
                    n += 16
                sp.dma_start(S["X"][:, :, :], L["x"].rearrange("b (t p) c -> p (b t) c", p=P)
                             ).then_inc(bcast_in, 16)
                n += 16
            sp.wait_ge(bcast_in, n)

        @block.gpsimd
        def _(pool):
            if l == 0:
                pool.memset(S["neg_half"][:, :], -0.5)
                pool.memset(S["ident"][:, :], 0.0).then_inc(ident_step, 1)
                pool.wait_ge(ident_step, 1)
                pool.affine_select(out=S["ident"][:, :], in_=S["ident"][:, :], compare_op=ALU.not_equal,
                                   fill=1.0, base=0, pattern=[[-1, P]], channel_multiplier=1
                                   ).then_inc(ident_step, 1)
                pool.wait_ge(ident_step, 2)
                pool.memset(S["condT"][CR:CR + 1, 2, :], 1.0).then_inc(ct_ones, 1)

        @block.scalar
        def _(act):
            if l == 0:
                act.wait_ge(cond_in, 16)
                act.activation(cond_silu[:, :], cond[:, :], ACT.Silu).then_inc(silu_done, 1)
            for n in range(4):
                act.wait_ge(mod_ps, n + 1)
                act.activation(mod[:, HALF * n:HALF * n + HALF], ps_mod[0:B, n, 0:HALF], ACT.Copy
                               ).then_inc(mod_done, 1)
            for i in range(2 * B):
                act.wait_ge(gate_ps, i + 1)
                act.activation(S["gates"][:, i // B, i % B, :], ps_gate[:, i % 2, 0:C], ACT.Copy
                               ).then_inc(gate_done, 1)

        @block.vector
        def _(dve):
            if l == 0:
                dve.wait_ge(ct_ps, 1)
                dve.tensor_copy(S["condT"][:, 0:2, :],
                                ps_small[:, 0, 0:8].rearrange("p (k b) -> p k b", k=2))
                dve.tensor_copy(S["condT"][0:CR, 2, :], ps_small[0:CR, 0, 8:12]).then_inc(ct_done, 1)
                dve.wait_ge(ident_step, 2)
            dve.tensor_copy(pick[:, :, :], S["ident"][0:B, 0:B].unsqueeze(2).to_broadcast([B, B, P])
                            ).then_inc(pick_done, 1)
            dve.wait_ge(attn_in, 16 * (12 if E > 1 else 8))
            split_weights(dve, split_step, 0, S["Wqkv"], raw_qkv[:, :, :], raw_qkv_rest[:, :])
            split_weights(dve, split_step, 2, S["Wproj"], raw_proj[:, :, :], raw_proj_rest[:, :])
            if E > 1:
                split_weights(dve, split_step, 4, S["Wgate"], raw_gate[:, :, :], raw_gate_rest[:, :])
            dve.wait_ge(modt_ps, 1)
            for v in range(4):
                for k, rows in ((0, P), (1, P), (2, CR)):
                    src = ps_small[0:rows, 0, 16 + (3 * v + k) * 4:16 + (3 * v + k) * 4 + 4]
                    dst = S["modT"][0:rows, v, k, :]
                    if v % 2:
                        dve.tensor_scalar(dst, src, 1.0, None, ALU.add)
                    else:
                        dve.tensor_copy(dst, src)
            dve.tensor_copy(S["b1T"][:, 0:E * NHC], ps_small[:, 1, 0:E * NHC])

        @block.tensor
        def _(pe):
            ident = S["ident"]
            if l == 0:
                pe.wait_ge(ident_step, 2)
                pe.wait_ge(silu_done, 1)
                for k, rows in ((0, P), (1, P), (2, CR)):
                    mm = pe.transpose(ps_small[0:rows, 0, 4 * k:4 * k + 4],
                                      cond_silu[:, P * k:P * k + rows], ident[0:B, 0:B])
                mm.then_inc(ct_ps, 1)
                pe.wait_ge(ct_done, 1)
                pe.wait_ge(ct_ones, 1)
            pe.wait_ge(mod_in, 48)
            for n in range(4):
                cols = slice(HALF * n, HALF * n + HALF)
                for k in range(2):
                    pe.matmul(ps_mod[0:B, n, 0:HALF], S["condT"][:, k, :], wm[:, k, cols],
                              start=(k == 0), stop=False)
                pe.matmul(ps_mod[0:B, n, 0:HALF], S["condT"][0:CR + 1, 2, :], wm_rest[:, cols],
                          start=False, stop=True).then_inc(mod_ps, 1)
            pe.wait_ge(mod_done, 4)
            for v, part in enumerate((0, 1, 3, 4)):
                for k, rows in ((0, P), (1, P), (2, CR)):
                    at = 16 + (3 * v + k) * 4
                    pe.transpose(ps_small[0:rows, 0, at:at + 4],
                                 mod[:, C * part + P * k:C * part + P * k + rows], ident[0:B, 0:B])
            pe.wait_ge(rows_in, 16)
            pe.transpose(ps_small[:, 1, 0:E * NHC], b1_rows[:, :], ident[0:E * NHC, 0:E * NHC]
                         ).then_inc(modt_ps, 1)
            pe.wait_ge(pick_done, 1)
            for i in range(2 * B):
                if i >= 2:
                    pe.wait_ge(gate_done, i - 1)
                part = (2, 5)[i // B]
                pe.matmul(ps_gate[:, i % 2, 0:C], pick[:, i % B, :], mod[:, C * part:C * part + C],
                          start=True, stop=True).then_inc(gate_ps, 1)


def attention(nc, sem, sb, pb, L, S):
    l = L["l"]
    head_norm = l == 0
    X, ident = S["X"], S["ident"]
    Wqkv, Wproj, modT, gates = S["Wqkv"], S["Wproj"], S["modT"], S["gates"]
    SCALE = float(HD) ** -0.5
    ctx = ExitStack()
    with ctx:
        def t(name, shape, dt=F32):
            return sb(ctx, f"{name}_a{l}", shape, dt)

        stats = t("stats", [P, TB, 6])
        mean_var = t("mean_var", [P, TB, 2])
        var_eps = t("var_eps", [P, TB, 1])
        neg_mean = t("neg_mean", [P, TB, 1])
        rstd = t("rstd", [P, TB, 1])
        neg_mean_rstd = t("neg_mean_rstd", [P, TB, 1])
        xn = t("xn", [P, TB, C])
        xt = t("xt", [P, 2, NB])
        xt_rest = t("xt_rest", [CR, NB])
        XS = t("XS", [P, 5, NB], F32R)
        qk = t("qk", [P, 2, QKW])
        qk_cen = t("qk_cen", [P, 2, QKW])
        qk_sq = t("qk_sq", [P, QKW])
        h_sum = t("h_sum", [P, 2 * NH])
        h_mean = t("h_mean", [P, 2 * NH])
        h_var = t("h_var", [P, 2 * NH])
        h_v = t("h_v", [P, 2 * NH])
        h_rstd = t("h_rstd", [P, 2 * NH])
        QKN = t("QKN", [P, TB, 2 * NG, HD, HG])
        v_in = t("v_in", [P, TB, C])
        V = t("V", [P, TB, NH, HD + 1])
        src_hi = t("src_hi", [GC, 2 * NG, NB], F32R)
        src_lo = t("src_lo", [GC, 2 * NG, NB], F32R)
        zero_row = t("zero_row", [NH, P], F32R)
        zero_f = t("zero_f", [NH, P])
        QS = [t(f"QS{i}", [KS_ROWS, HG, NB], F32R) for i in range(2)]
        KS = [t(f"KS{i}", [KS_ROWS, HG, NB], F32R) for i in range(2)]
        neg_max = t("neg_max", [P, HG * TB])
        neg_max_rows = t("neg_max_rows", [HG * TB, P], F32R)
        probs = t("probs", [P, 2, HG, NB])
        OT = t("OT", [P, NB])
        rden = t("rden", [P, TB, HG])
        ON = t("ON", [P, TB, C])
        y = t("y", [P, TB, C])

        ps_shared = pb(ctx, f"ps_shared{l}", [P, 2, 512], F32)
        ps_max = pb(ctx, f"ps_max{l}", [P, 2, 512], F32)
        ps_exp = pb(ctx, f"ps_exp{l}", [P, 3, 512], F32)
        ps_out = pb(ctx, f"ps_out{l}", [P, 512], F32)

        def s(name):
            return sem(f"{name}_a{l}")

        inited = s("inited")
        parted = s("parted")
        stats_done = s("stats_done")
        mv_done = s("mv_done")
        ve_done = s("ve_done")
        rstd_done = s("rstd_done")
        coef_done = s("coef_done")
        xn_done = s("xn_done")
        xs_hi = s("xs_hi")
        xs_lo = s("xs_lo")
        xs_lo_rest = s("xs_lo_rest")
        full = [s("full0"), s("full1")]
        free = [s("free0"), s("free1")]
        qk_done = s("qk_done")
        h_sum_done = s("h_sum_done")
        h_mean_done = s("h_mean_done")
        cen_done = s("cen_done")
        sq_done = s("sq_done")
        h_var_done = s("h_var_done")
        h_v_done = s("h_v_done")
        h_rstd_done = s("h_rstd_done")
        cen_scaled = s("cen_scaled")
        qkn_done = s("qkn_done")
        v_ones = s("v_ones")
        v_done = s("v_done")
        hi_done = s("hi_done")
        loaded = [s("loaded0"), s("loaded1")]
        max_full = s("max_full")
        max_done = s("max_done")
        m_loaded = s("m_loaded")
        exp_full = s("exp_full")
        exp_done = s("exp_done")
        pv_done = s("pv_done")
        ot_done = s("ot_done")
        rden_done = s("rden_done")
        o_hi = s("o_hi")
        y_gated = s("y_gated")
        x_done = s("x_done")

        LOADS = 7 * 16

        block = ctx.enter_context(nc.Block())

        @block.tensor
        def _(pe):
            def fill(use, b, last=False):
                n, k = count(use, b, last), USES.bank(use)
                if not isinstance(n, int) or n > 1:
                    pe.wait_ge(free[k], n - 1)
                return ps_shared[:, k, :], full[k]

            def x_transposes(b, nb):
                pe.wait_ge(xn_done, nb * TB + TB)
                for c, (use, rows) in enumerate((("xA", P), ("xB", P), ("xC", CR))):
                    ps, filled = fill(use, b)
                    for i in range(TB):
                        mm = pe.transpose(ps[0:rows, P * i:P * i + P],
                                          xn[:, i, P * c:P * c + rows], ident[:, :])
                    mm.then_inc(filled, 1)

            def qkv(b, nb, i):
                if i == 0:
                    pe.wait_ge(xs_hi, nb * 4 + 4)
                    pe.wait_ge(xs_lo, nb * 2 + 2)
                    pe.wait_ge(xs_lo_rest, nb + 1)
                for h in range(2):
                    ps, filled = fill(f"qkv{i}{'ab'[h]}", b)
                    for n, (w, x) in enumerate(PAIRS):
                        r = rows_of(w)
                        mm = pe.matmul(ps[:, 0:HALF], XS[0:r, x, P * i:P * i + P],
                                       Wqkv[0:r, w, HALF * h:HALF * h + HALF],
                                       start=(n == 0), stop=(n == len(PAIRS) - 1))
                    mm.then_inc(filled, 1)

            def qk_transposes(b, nb, g):
                for s_, name in enumerate("qk"):
                    ps, filled = fill(f"{name}{g}", b)
                    for i in range(TB):
                        mm = pe.transpose(ps[0:GC, P * i:P * i + P],
                                          QKN[:, i, NG * s_ + g, :, :].rearrange("p d j -> p (d j)"),
                                          ident[:, :])
                    mm.then_inc(filled, 1)

            def max_scores(g, j, i):
                return pe.matmul(ps_max[:, (j * TB + i) % 2, :], QS[g % 2][:, j, P * i:P * i + P],
                                 KS[g % 2][:, j, :], start=True, stop=True)

            def max_rows(use, b, n):
                ps, filled = fill(use, b)
                pe.wait_ge(max_done, n * 16 + 16)
                pe.transpose(ps[0:HG * TB, 0:P], neg_max[:, :], ident[:, :]).then_inc(filled, 1)

            def values(b, g, i):
                for j in range(HG):
                    pe.wait_ge(exp_done, b * 64 + (16 * g + 4 * i + j + 1))
                    mm = pe.matmul(ps_out[32 * j:32 * j + HD + 1, :], V[:, i, HG * g + j, :],
                                   probs[:, i % 2, j, :], start=(i == 0), stop=(i == TB - 1))
                mm.then_inc(pv_done, 1)

            def batch(b, last):
                nb = b + 1
                pe.wait_ge(v_done, b + 1)
                for g in range(NG):
                    ahead = (g + 1) % NG
                    has_ahead = not (last and g == NG - 1)
                    pe.wait_ge(m_loaded, b * 64 + (16 * g + 16))
                    if has_ahead:
                        pe.wait_ge(loaded[ahead % 2], b * (2 * LOADS) + LOADS * ((g + 1) // 2 + 1))
                    for i in range(TB):
                        for j in range(HG):
                            n = HG * i + j
                            if n >= 3:
                                pe.wait_ge(exp_done, b * 64 + (16 * g + n - 2))
                            pe.matmul(ps_exp[:, n % 3, :], KS[g % 2][:, j, P * i:P * i + P],
                                      QS[g % 2][:, j, :], start=True, stop=True).then_inc(exp_full, 1)
                            if has_ahead:
                                if n >= 2:
                                    pe.wait_ge(max_done, b * 64 + (16 * (g + 1) + n - 1))
                                max_scores(ahead, i, j).then_inc(max_full, 1)
                        if i >= 1:
                            values(b, g, i - 1)
                        if not last and (g, i) == (0, 1):
                            x_transposes(b, nb)
                        if not last and (g, i) == (2, 2):
                            pe.wait_ge(qkn_done, nb * TB + TB)
                            qk_transposes(b, nb, 0)
                    if has_ahead:
                        pe_n = b * 4 + (g + 1)
                        ps, filled = fill(f"max{g}", b, last)
                        pe.wait_ge(max_done, b * 64 + (16 * (g + 1) + 16))
                        pe.transpose(ps[0:HG * TB, 0:P], neg_max[:, :], ident[:, :]).then_inc(filled, 1)
                    values(b, g, TB - 1)
                    if not last and g < 2:
                        qkv(b, nb, 2 * g)
                        qkv(b, nb, 2 * g + 1)
                    if not last and g == 2:
                        for h in range(1, NG):
                            qk_transposes(b, nb, h)
                    ps, filled = fill(f"o{g}", b, last)
                    pe.wait_ge(ot_done, b * 4 + (g + 1))
                    for i in range(TB):
                        mm = pe.transpose(ps[:, P * i:P * i + P], OT[:, P * i:P * i + P], ident[:, :])
                    mm.then_inc(filled, 1)
                pe.wait_ge(free[USES.bank("o3")], count("o3", b, last))
                for c, (use, rows) in enumerate((("oA", P), ("oB", P), ("oC", CR))):
                    ps, filled = fill(use, b, last)
                    for i in range(TB):
                        mm = pe.transpose(ps[0:rows, P * i:P * i + P], ON[:, i, P * c:P * c + rows],
                                          ident[:, :])
                    mm.then_inc(filled, 1)
                for use in ("oA", "oB", "oC"):
                    pe.wait_ge(free[USES.bank(use)], count(use, b, last))
                for i in range(TB):
                    ps, filled = fill(f"proj{i}", b, last)
                    for n, (w, x) in enumerate(PAIRS):
                        r = rows_of(w)
                        mm = pe.matmul(ps[:, 0:C], XS[0:r, x, P * i:P * i + P], Wproj[0:r, w, :],
                                       start=(n == 0), stop=(n == len(PAIRS) - 1))
                    mm.then_inc(filled, 1)

            pe.wait_ge(inited, 2)
            x_transposes(None, 0)
            for i in range(TB):
                qkv(None, 0, i)
            pe.wait_ge(qkn_done, TB)
            for g in range(NG):
                qk_transposes(None, 0, g)
            pe.wait_ge(loaded[0], LOADS)
            for j in range(HG):
                for i in range(TB):
                    if j * TB + i >= 2:
                        pe.wait_ge(max_done, j * TB + i - 1)
                    max_scores(0, j, i).then_inc(max_full, 1)
            max_rows("max3", None, 0)
            with pe.Fori(0, B - 1) as b:
                batch(b, False)
            batch(B - 1, True)

        @block.scalar
        def _(act):
            def normalise(nb):
                act.wait_ge(coef_done, nb + 1)
                act.sem_inc(parted, 1)
                for i in range(TB):
                    act.activation(xn[:, i:i + 1, :], X[:, bass.ds(nb * TB + i, 1), :], ACT.Identity,
                                   bias=neg_mean_rstd[:, i, :], scale=rstd[:, i, :]).then_inc(xn_done, 1)

            def x_hi(b):
                for c, use in enumerate(("xA", "xB")):
                    act.wait_ge(free[USES.bank(use)], count(use, b))
                    act.activation(XS[:, c, :], xt[:, c, :], ACT.Copy).then_inc(xs_hi, 1)
                act.wait_ge(free[USES.bank("xC")], count("xC", b))
                act.activation(XS[0:CR, 4, :], xt_rest[:, :], ACT.Copy).then_inc(xs_hi, 1)
                act.activation(XS[2 * CR:3 * CR, 4, :], xt_rest[:, :], ACT.Copy).then_inc(xs_hi, 1)

            def squares(nb, i):
                if head_norm:
                    if not (isinstance(nb, int) and nb == 0) or i >= 1:
                        act.wait_ge(h_var_done, nb * TB + i)
                    act.wait_ge(cen_done, nb * TB + (i + 1))
                    act.activation(qk_sq[:, :], qk_cen[:, i % 2, :], ACT.Square).then_inc(sq_done, 1)

            def qk_hi(b, nb, g):
                for s_, name in enumerate("qk"):
                    use = f"{name}{g}"
                    if b is not None and s_ == 0:
                        act.wait_ge(loaded[g % 2], b * (2 * LOADS) + LOADS * (g // 2 + 1))
                    act.wait_ge(full[USES.bank(use)], count(use, b))
                    act.activation(src_hi[:, NG * s_ + g, :], ps_shared[0:GC, USES.bank(use), :],
                                   ACT.Copy).then_inc(hi_done, 1)

            def max_rows(use, b, n, last=False):
                k = USES.bank(use)
                if b is not None:
                    act.wait_ge(m_loaded, n * 16)
                act.wait_ge(full[k], count(use, b, last))
                act.activation(neg_max_rows[:, :], ps_shared[0:HG * TB, k, 0:P], ACT.Copy
                               ).then_inc(free[k], 1)

            def batch(b, last):
                nb = b + 1
                for g in range(NG):
                    for i in range(TB):
                        if i >= 2:
                            act.wait_ge(pv_done, b * 16 + (4 * g + i - 1))
                        for j in range(HG):
                            n = HG * i + j
                            act.wait_ge(exp_full, b * 64 + (16 * g + n + 1))
                            act.activation(probs[:, i % 2, j, :], ps_exp[:, n % 3, :], ACT.Exp,
                                           scale=SCALE).then_inc(exp_done, 1)
                        if not last and (g, i) == (0, 0):
                            normalise(nb)
                        if not last and (g, i) == (0, 2):
                            x_hi(b)
                        if not last and (g, i) in ((1, 0), (1, 1)):
                            squares(nb, i)
                        if not last and (g, i) == (2, 0):
                            squares(nb, 2)
                            squares(nb, 3)
                        if not last and (g, i) == (2, 3):
                            qk_hi(b, nb, 0)
                    if not (last and g == NG - 1):
                        max_rows(f"max{g}", b, b * 4 + (g + 1), last)
                    act.wait_ge(pv_done, b * 16 + (4 * g + 4))
                    act.activation(OT[:, :], ps_out[:, :], ACT.Copy).then_inc(ot_done, 1)
                    if not last and g == 2:
                        for h in range(1, NG):
                            qk_hi(b, nb, h)
                for c, use in enumerate(("oA", "oB")):
                    k = USES.bank(use)
                    act.wait_ge(full[k], count(use, b, last))
                    act.activation(XS[:, c, :], ps_shared[:, k, :], ACT.Copy).then_inc(o_hi, 1)
                k = USES.bank("oC")
                act.wait_ge(full[k], count("oC", b, last))
                act.activation(XS[0:CR, 4, :], ps_shared[0:CR, k, :], ACT.Copy).then_inc(o_hi, 1)
                act.activation(XS[2 * CR:3 * CR, 4, :], ps_shared[0:CR, k, :], ACT.Copy).then_inc(o_hi, 1)

            normalise(0)
            x_hi(None)
            for i in range(TB):
                squares(0, i)
            for g in range(NG):
                qk_hi(None, 0, g)
            max_rows("max3", None, 0)
            with act.Fori(0, B - 1) as b:
                batch(b, False)
            batch(B - 1, True)

        @block.vector
        def _(dve):
            def coefficients(nb):
                for i in range(TB):
                    st = dve.bn_stats(stats[:, i:i + 1, :], X[:, bass.ds(nb * TB + i, 1), :])
                st.then_inc(stats_done, 1)
                dve.wait_ge(stats_done, nb + 1)
                dve.sem_inc(parted, 1)
                for i in range(TB):
                    mv = dve.bn_aggr(mean_var[:, i, :], stats[:, i, :])
                mv.then_inc(mv_done, 1)

            def modulate(b, nb, use, c):
                k = USES.bank(use)
                dst = xt_rest[:, :] if c == 2 else xt[:, c, :]
                rows = CR if c == 2 else P
                dve.wait_ge(full[k], count(use, b))
                dve.sem_inc(parted, 1)
                dve.tensor_scalar(dst, ps_shared[0:rows, k, :],
                                  modT[0:rows, 1, c, bass.ds(nb, 1)],
                                  modT[0:rows, 0, c, bass.ds(nb, 1)],
                                  ALU.mult, ALU.add).then_inc(free[k], 1)

            def modulated(b, nb):
                for c, use in enumerate(("xA", "xB", "xC")):
                    modulate(b, nb, use, c)

            def x_lo_rest(nb):
                dve.wait_ge(xs_hi, nb * 4 + 4)
                dve.tensor_tensor(XS[CR:2 * CR, 4, :], xt_rest[:, :], f(XS[0:CR, 4, :]),
                                  ALU.subtract).then_inc(xs_lo_rest, 1)

            def qkv(b, nb, i):
                ka, kb = USES.bank(f"qkv{i}a"), USES.bank(f"qkv{i}b")
                na, nb_ = count(f"qkv{i}a", b), count(f"qkv{i}b", b)
                cut = HALF // GC
                bias = S["bqkv"]
                dve.wait_ge(full[ka], na)
                if head_norm:
                    dve.tensor_tensor(qk[:, i % 2, 0:HALF], ps_shared[:, ka, 0:HALF], bias[:, 0:HALF],
                                      ALU.add).then_inc(free[ka], 1)
                else:
                    dve.tensor_tensor(
                        QKN[:, i, 0:cut, :, :].rearrange("p g d j -> p g j d"),
                        ps_shared[:, ka, 0:HALF].rearrange("p (g j d) -> p g j d", g=cut, j=HG),
                        bias[:, 0:HALF].rearrange("p (g j d) -> p g j d", g=cut, j=HG),
                        ALU.add).then_inc(free[ka], 1)
                dve.wait_ge(full[kb], nb_)
                rest = QKW - HALF
                if head_norm:
                    dve.tensor_tensor(qk[:, i % 2, HALF:QKW], ps_shared[:, kb, 0:rest],
                                      bias[:, HALF:QKW], ALU.add).then_inc(qk_done, 1)
                else:
                    dve.tensor_tensor(
                        QKN[:, i, cut:2 * NG, :, :].rearrange("p g d j -> p g j d"),
                        ps_shared[:, kb, 0:rest].rearrange("p (g j d) -> p g j d", g=2 * NG - cut, j=HG),
                        bias[:, HALF:QKW].rearrange("p (g j d) -> p g j d", g=2 * NG - cut, j=HG),
                        ALU.add).then_inc(qkn_done, 1)
                if b is not None:
                    dve.wait_ge(v_done, nb)
                dve.tensor_tensor(v_in[:, i, :], ps_shared[:, kb, rest:HALF], bias[:, QKW:3 * C],
                                  ALU.add).then_inc(free[kb], 1)
                if head_norm:
                    n = nb * TB + (i + 1)
                    dve.wait_ge(qk_done, n)
                    dve.reduce_sum(h_sum[:, :], qk[:, i % 2, :].rearrange("p (h d) -> p h d", d=HD),
                                   AX).then_inc(h_sum_done, 1)
                    dve.wait_ge(h_sum_done, n)
                    if b is not None or i > 0:
                        dve.wait_ge(cen_done, n - 1)
                    dve.tensor_scalar(h_mean[:, :], h_sum[:, :], 1.0 / HD, None, ALU.mult
                                      ).then_inc(h_mean_done, 1)

            def head_squares(nb, i):
                n = nb * TB + (i + 1)
                if not isinstance(n, int) or n > 1:
                    dve.wait_ge(h_v_done, n - 1)
                dve.wait_ge(sq_done, n)
                dve.reduce_sum(h_var[:, :], qk_sq[:, :].rearrange("p (h d) -> p h d", d=HD),
                               AX).then_inc(h_var_done, 1)

            def head_gain(nb, i):
                dve.wait_ge(cen_scaled, nb * TB + (i + 1))
                for s_ in range(2):
                    gn = dve.tensor_tensor(
                        QKN[:, i, NG * s_:NG * s_ + NG, :, :].rearrange("p g d j -> p g j d"),
                        qk_cen[:, i % 2, C * s_:C * s_ + C].rearrange("p (g j d) -> p g j d", g=NG, j=HG),
                        S["gain"][:, s_, :].unsqueeze(1).unsqueeze(1).to_broadcast([P, NG, HG, HD]),
                        ALU.mult)
                gn.then_inc(qkn_done, 1)

            def qk_lo(b, nb, g):
                for s_, name in enumerate("qk"):
                    use = f"{name}{g}"
                    k = USES.bank(use)
                    dve.wait_ge(hi_done, nb * 8 + (2 * g + s_ + 1))
                    dve.tensor_tensor(src_lo[:, NG * s_ + g, :], ps_shared[0:GC, k, :],
                                      f(src_hi[:, NG * s_ + g, :]), ALU.subtract).then_inc(free[k], 1)

            def maxima(n):
                dve.reduce_max(neg_max[:, n:n + 1], ps_max[:, n % 2, :], AX, negate=True
                               ).then_inc(max_done, 1)

            def batch(b, last):
                nb = b + 1
                for g in range(NG):
                    has_ahead = not (last and g == NG - 1)
                    for i in range(TB):
                        if has_ahead:
                            for j in range(HG):
                                n = HG * i + j
                                dve.wait_ge(max_full, b * 64 + (16 * (g + 1) + n + 1))
                                maxima(n)
                        if last:
                            continue
                        if (g, i) == (0, 0):
                            coefficients(nb)
                        if (g, i) == (0, 1):
                            modulated(b, nb)
                        if (g, i) == (0, 2):
                            x_lo_rest(nb)
                        if head_norm:
                            if (g, i) in ((1, 0), (1, 1)):
                                head_squares(nb, i)
                                head_gain(nb, i)
                            if (g, i) == (2, 0):
                                head_squares(nb, 2)
                                head_squares(nb, 3)
                            if (g, i) == (2, 1):
                                head_gain(nb, 2)
                                head_gain(nb, 3)
                        if (g, i) == (2, 3):
                            qk_lo(b, nb, 0)
                    if not last and g < 2:
                        qkv(b, nb, 2 * g)
                        qkv(b, nb, 2 * g + 1)
                    if not last and g == 2:
                        for h in range(1, NG):
                            qk_lo(b, nb, h)
                    use = f"o{g}"
                    k = USES.bank(use)
                    ps = ps_shared[:, k, :].rearrange("p (i j r) -> p i j r", i=TB, j=HG)
                    dve.wait_ge(full[k], count(use, b, last))
                    dve.reciprocal(rden[:, :, :].unsqueeze(3), ps[:, :, :, HD:HD + 1]).then_inc(rden_done, 1)
                    dve.wait_ge(rden_done, b * 4 + (g + 1))
                    dve.tensor_tensor(ON[:, :, GC * g:GC * g + GC].rearrange("p i (j d) -> p i j d", j=HG),
                                      ps[:, :, :, 0:HD],
                                      rden[:, :, :].unsqueeze(3).to_broadcast([P, TB, HG, HD]),
                                      ALU.mult).then_inc(free[k], 1)
                for c, use in enumerate(("oA", "oB")):
                    k = USES.bank(use)
                    dve.wait_ge(o_hi, b * 4 + (c + 1))
                    dve.tensor_tensor(XS[:, 2 + c, :], ps_shared[:, k, :], f(XS[:, c, :]),
                                      ALU.subtract).then_inc(free[k], 1)
                k = USES.bank("oC")
                dve.wait_ge(o_hi, b * 4 + 4)
                dve.tensor_tensor(XS[CR:2 * CR, 4, :], ps_shared[0:CR, k, :], f(XS[0:CR, 4, :]),
                                  ALU.subtract).then_inc(free[k], 1)
                if last:
                    dve.wait_ge(x_done, b * TB)
                for i in range(TB):
                    k = USES.bank(f"proj{i}")
                    dve.wait_ge(full[k], count(f"proj{i}", b, last))
                    dve.tensor_tensor(y[:, i, :], ps_shared[:, k, 0:C], S["bproj"][:, :],
                                      ALU.add).then_inc(free[k], 1)

            dve.memset(ps_out[:, :], 0.0)
            for q, k in zip(QS, KS):
                dve.memset(f(q[:, :, :]), 0.0)
                dve.memset(f(k[:, :, :]), 1.0)
            dve.memset(zero_f[:, :], 0.0).then_inc(inited, 1)
            dve.wait_ge(inited, 1)
            dve.tensor_copy(zero_row[:, :], zero_f[:, :]).then_inc(inited, 1)
            coefficients(0)
            modulated(None, 0)
            x_lo_rest(0)
            for i in range(TB):
                qkv(None, 0, i)
                if head_norm and i >= 1:
                    head_squares(0, i - 1)
                    head_gain(0, i - 1)
            if head_norm:
                head_squares(0, TB - 1)
                head_gain(0, TB - 1)
            for g in range(NG):
                qk_lo(None, 0, g)
            for n in range(HG * TB):
                dve.wait_ge(max_full, n + 1)
                maxima(n)
            with dve.Fori(0, B - 1) as b:
                batch(b, False)
            batch(B - 1, True)

        @block.gpsimd
        def _(pool):
            def coefficients(nb):
                pool.wait_ge(mv_done, nb + 1)
                pool.sem_inc(parted, 1)
                pool.tensor_scalar(var_eps[:, :, :], mean_var[:, :, 1:2], EPS, 1.0, ALU.add, ALU.mult)
                pool.tensor_scalar(neg_mean[:, :, :], mean_var[:, :, 0:1], -1.0, 1.0, ALU.mult, ALU.mult
                                   ).then_inc(ve_done, 1)
                pool.wait_ge(ve_done, nb + 1)
                pool.tensor_tensor(rstd[:, :, :], var_eps[:, :, :],
                                   S["neg_half"][:, 0:TB].unsqueeze(2), ALU.pow).then_inc(rstd_done, 1)
                pool.wait_ge(rstd_done, nb + 1)
                pool.tensor_tensor(neg_mean_rstd[:, :, :], neg_mean[:, :, :], rstd[:, :, :],
                                   ALU.mult).then_inc(coef_done, 1)

            def x_lo(nb):
                for c in range(2):
                    pool.wait_ge(xs_hi, nb * 4 + (c + 1))
                    pool.tensor_tensor(XS[:, 2 + c, :], xt[:, c, :], f(XS[:, c, :]),
                                       ALU.subtract).then_inc(xs_lo, 1)

            def centre(b, nb, i):
                n = nb * TB + i
                pool.wait_ge(h_mean_done, n + 1)
                if b is not None or i >= 2:
                    pool.wait_ge(qkn_done, n - 1)
                pool.tensor_tensor(
                    qk_cen[:, i % 2, :].rearrange("p (h d) -> p h d", d=HD),
                    qk[:, i % 2, :].rearrange("p (h d) -> p h d", d=HD),
                    h_mean[:, :].unsqueeze(2).to_broadcast([P, 2 * NH, HD]),
                    ALU.subtract).then_inc(cen_done, 1)

            def scale_heads(nb, i):
                n = nb * TB + (i + 1)
                pool.wait_ge(h_var_done, n)
                pool.sem_inc(parted, 1)
                pool.tensor_scalar(h_v[:, :], h_var[:, :], 1.0 / HD, EPS, ALU.mult, ALU.add
                                   ).then_inc(h_v_done, 1)
                pool.wait_ge(h_v_done, n)
                pool.tensor_tensor(h_rstd[:, :], h_v[:, :], S["neg_half"][:, :], ALU.pow
                                   ).then_inc(h_rstd_done, 1)
                pool.wait_ge(h_rstd_done, n)
                pool.tensor_tensor(
                    qk_cen[:, i % 2, :].rearrange("p (h d) -> p h d", d=HD),
                    qk_cen[:, i % 2, :].rearrange("p (h d) -> p h d", d=HD),
                    h_rstd[:, :].unsqueeze(2).to_broadcast([P, 2 * NH, HD]),
                    ALU.mult).then_inc(cen_scaled, 1)

            def copy_v(b, nb):
                pool.wait_ge(free[1], count("qkv3b", b))
                if b is not None:
                    pool.wait_ge(pv_done, nb * 16)
                    pool.sem_inc(parted, 1)
                pool.tensor_scalar(V[:, :, :, 0:HD].rearrange("p i h d -> p (i h) d"),
                                   v_in[:, :, :].rearrange("p i (h d) -> p (i h) d", d=HD),
                                   1.0, 1.0, ALU.mult, ALU.mult).then_inc(v_done, 1)

            def batch(b, last):
                nb = b + 1
                if not last:
                    coefficients(nb)
                    x_lo(nb)
                    if head_norm:
                        centre(b, nb, 0)
                        centre(b, nb, 1)
                        scale_heads(nb, 0)
                        scale_heads(nb, 1)
                        centre(b, nb, 2)
                        centre(b, nb, 3)
                        scale_heads(nb, 2)
                        scale_heads(nb, 3)
                    copy_v(b, nb)
                for i in range(TB):
                    k = USES.bank(f"proj{i}")
                    pool.wait_ge(free[k], count(f"proj{i}", b, last))
                    pool.sem_inc(parted, 1)
                    pool.tensor_tensor(y[:, i:i + 1, :], y[:, i:i + 1, :],
                                       gates[:, 0, bass.ds(b, 1), :], ALU.mult).then_inc(y_gated, 1)
                    pool.wait_ge(y_gated, b * TB + (i + 1))
                    pool.sem_inc(parted, 1)
                    x_tile = X[:, bass.ds(b * TB + i, 1), :]
                    pool.tensor_tensor(x_tile, x_tile, y[:, i:i + 1, :], ALU.add).then_inc(x_done, 1)

            pool.memset(V[:, :, :, :], 1.0).then_inc(v_ones, 1)
            pool.wait_ge(v_ones, 1)
            coefficients(0)
            x_lo(0)
            if head_norm:
                for i in range(TB):
                    centre(None, 0, i)
                    scale_heads(0, i)
            copy_v(None, 0)
            with pool.Fori(0, B - 1) as b:
                batch(b, False)
            batch(B - 1, True)

        @block.sync
        def _(sp):
            def parts_ready(b, g):
                for name in "qk":
                    sp.wait_ge(free[USES.bank(f"{name}{g}")], count(f"{name}{g}", b))
                    sp.sem_inc(parted, 1)

            def max_row(use, b, g, last=False):
                k = USES.bank(use)
                sp.wait_ge(free[k], count(use, b, last))
                sp.sem_inc(parted, 1)
                sp.dma_start(f(QS[g % 2][M_ROW:M_ROW + 1, :, :]), f(neg_max_rows[:, :])).then_inc(m_loaded, 16)

            def batch(b, last):
                nb = b + 1
                for g in range(NG):
                    if not (last and g == NG - 1):
                        max_row(f"max{g}", b, g + 1, last)
                    ahead = g + 2
                    if ahead < NG or not last:
                        sp.wait_ge(exp_full, b * 64 + (16 * g + 16))
                        sp.sem_inc(parted, 1)
                        if ahead >= NG:
                            parts_ready(b, ahead - NG)
                        stacks(ahead % NG)
                if not last:
                    parts_ready(b, NG - 1)

            def stacks(g):
                par = g % 2
                for dst, at, src, s_ in ((QS, 0, src_hi, 0), (QS, 1, src_lo, 0), (QS, 2, src_hi, 0),
                                         (KS, 0, src_hi, 1), (KS, 1, src_hi, 1), (KS, 2, src_lo, 1)):
                    sp.dma_start(f(dst[par][HD * at:HD * at + HD, :, :]), f(src[:, NG * s_ + g, :])
                                 ).then_inc(loaded[par], 16)
                sp.dma_start(f(QS[par][M_ROW:M_ROW + 1, :, :]), f(zero_row[:, :])).then_inc(loaded[par], 16)

            sp.wait_ge(inited, 2)
            for g in range(2):
                parts_ready(None, g)
                stacks(g)
            parts_ready(None, NG - 1)
            max_row("max3", None, 0)
            with sp.Fori(0, B - 1) as b:
                batch(b, False)
            batch(B - 1, True)


def mlp(nc, sem, sb, pb, L, S):
    l, E = L["l"], L["E"]
    X, ident, modT, gates = S["X"], S["ident"], S["modT"], S["gates"]
    ctx = ExitStack()
    with ctx:
        def t(name, shape, dt=F32):
            return sb(ctx, f"{name}_m{l}", shape, dt)

        n_slots = min(E, 2)
        stats = t("stats", [P, TB, 6])
        mean_var = t("mean_var", [P, TB, 2])
        var_eps = t("var_eps", [P, TB, 1])
        neg_mean = t("neg_mean", [P, TB, 1])
        rstd = t("rstd", [P, TB, 1])
        neg_mean_rstd = t("neg_mean_rstd", [P, TB, 1])
        xn = t("xn", [P, TB, C])
        xt = t("xt", [P, 2, NB])
        xt_rest = t("xt_rest", [CR, NB])
        XS = t("XS", [P, 5, B * NB], F32R)
        raw = t("raw", [P, 2, HID])
        W1 = [t(f"W1_{i}", [P, 5, HID], F32R) for i in range(n_slots)]
        W2 = [t(f"W2_{i}", [P, 2, NHC, C], F32R) for i in range(n_slots)]
        G = t("G", [P, 3, NB])
        HHI = t("HHI", [P, 3, NB], F32R)
        HLO = t("HLO", [P, 3, NB], F32R)
        y = t("y", [P, TB, C])
        logits = t("logits", [P, TB, 4])
        beats = t("beats", [P, 6, TB])
        rank = t("rank", [P, TB, 4])
        best = t("best", [P, TB])
        shifted = t("shifted", [P, TB, 4])
        ex = t("ex", [P, TB, 4])
        picked = t("picked", [P, TB, 4])
        total = t("total", [P, TB])
        rtotal = t("rtotal", [P, TB])
        cw = t("cw", [P, T, 4])

        ps_h = pb(ctx, f"ps_h{l}", [P, 3, 512], F32)
        ps_y = pb(ctx, f"ps_y{l}", [P, TB, 512], F32)
        ps_ln = pb(ctx, f"ps_ln{l}", [P, 512], F32)

        def s(name):
            return sem(f"{name}_m{l}")

        parted = s("parted")
        chain = s("chain")
        stats_done = s("stats_done")
        mv_done = s("mv_done")
        ve_done = s("ve_done")
        rstd_done = s("rstd_done")
        coef_done = s("coef_done")
        xn_done = s("xn_done")
        ln_full = s("ln_full")
        ln_free = s("ln_free")
        xs_hi = s("xs_hi")
        xs_lo = s("xs_lo")
        xs_lo_rest = s("xs_lo_rest")
        shifted_done = s("shifted_done")
        ex_done = s("ex_done")
        cw_done = s("cw_done")
        raw_in = [s("raw_in0"), s("raw_in1")]
        hi_split = s("hi_split")
        split_done = s("split_done")
        h_full = s("h_full")
        gelu_done = s("gelu_done")
        h_hi = s("h_hi")
        h_lo = s("h_lo")
        h_used = s("h_used")
        y_full = s("y_full")
        y_free = s("y_free")
        y_gated = s("y_gated")
        x_done = s("x_done")
        out_done = s("out_done")

        LN_USES = 4 if E > 1 else 3
        RUNS = [(0, 4), (4, 8), (8, NHC)]
        NPIECES = 3 + len(RUNS)
        PIECE_DMAS = [1, 1, 3, 1, 1, 1]

        def arrived(e, n):
            slot = n % 2
            before = sum(PIECE_DMAS[m] for m in range(NPIECES) if m % 2 == slot) * e
            return slot, 16 * (before + sum(PIECE_DMAS[m] for m in range(n + 1) if m % 2 == slot))

        block = ctx.enter_context(nc.Block())

        @block.sync
        def _(sp):
            for e in range(E):
                w1, w2 = L["w1"][e], L["w2"][e]
                for n in range(NPIECES):
                    if e * NPIECES + n >= 2:
                        sp.wait_ge(split_done, e * NPIECES + n - 1)
                    slot = n % 2
                    if n < 2:
                        sp.dma_start(raw[:, slot, :], w1[P * n:P * n + P, :]).then_inc(raw_in[slot], 16)
                    elif n == 2:
                        for r in range(3):
                            sp.dma_start(raw[CR * r:CR * r + CR, slot, :], w1[2 * P:C, :]
                                         ).then_inc(raw_in[slot], 16)
                    else:
                        a, z = RUNS[n - 3]
                        sp.dma_start(raw[:, slot, 0:C * (z - a)].rearrange("p (k n) -> p k n", n=C),
                                     w2[P * a:P * z, :].rearrange("(k p) n -> p k n", p=P)
                                     ).then_inc(raw_in[slot], 16)
            if L["out"] is not None:
                for b in range(B):
                    sp.wait_ge(x_done, ((E - 1) * B + b + 1) * TB)
                    sp.dma_start(L["out"][b].rearrange("(t p) c -> p t c", p=P),
                                 X[:, TB * b:TB * b + TB, :]).then_inc(out_done, 16)
                sp.wait_ge(out_done, 16 * B)

        def split_piece(eng, e, n, copy):
            k, m = e % n_slots, e * NPIECES + n
            slot, there = arrived(e, n)
            eng.wait_ge(raw_in[slot], there)
            if n < 3:
                r = rows_of(4) if n == 2 else P
                src = raw[0:r, slot, :]
                hi = W1[k][0:r, (0, 1, 4)[n], :]
                lo_src, lo_hi, lo = src, hi, W1[k][:, 2 + n, :] if n < 2 else None
                if n == 2:
                    lo_src, lo_hi = raw[2 * CR:3 * CR, slot, :], W1[k][2 * CR:3 * CR, 4, :]
                    lo = lo_hi
            else:
                a, z = RUNS[n - 3]
                lo_src = src = raw[:, slot, 0:C * (z - a)].rearrange("p (k n) -> p k n", n=C)
                lo_hi = hi = W2[k][:, 0, a:z, :]
                lo = W2[k][:, 1, a:z, :]
            if n == 3:
                eng.wait_ge(split_done, m)
            copy(hi, src).then_inc(hi_split, 1)
            eng.wait_ge(hi_split, m + 1)
            eng.tensor_tensor(lo, lo_src, f(lo_hi), ALU.subtract).then_inc(split_done, 1)

        @block.gpsimd
        def _(pool):
            def coefficients(nb):
                pool.wait_ge(mv_done, nb + 1)
                if nb >= 1:
                    pool.wait_ge(xn_done, TB * nb)
                pool.tensor_scalar(var_eps[:, :, :], mean_var[:, :, 1:2], EPS, 1.0, ALU.add, ALU.mult)
                pool.tensor_scalar(neg_mean[:, :, :], mean_var[:, :, 0:1], -1.0, 1.0, ALU.mult, ALU.mult
                                   ).then_inc(ve_done, 1)
                pool.wait_ge(ve_done, nb + 1)
                pool.tensor_tensor(rstd[:, :, :], var_eps[:, :, :],
                                   S["neg_half"][:, 0:TB].unsqueeze(2), ALU.pow).then_inc(rstd_done, 1)
                pool.wait_ge(rstd_done, nb + 1)
                pool.tensor_tensor(neg_mean_rstd[:, :, :], neg_mean[:, :, :], rstd[:, :, :],
                                   ALU.mult).then_inc(coef_done, 1)

            def x_lo(b):
                for c in range(2):
                    pool.wait_ge(xs_hi, 4 * b + c + 1)
                    pool.tensor_tensor(XS[:, 2 + c, NB * b:NB * b + NB], xt[:, c, :],
                                       f(XS[:, c, NB * b:NB * b + NB]), ALU.subtract).then_inc(xs_lo, 1)

            coefficients(0)
            for b in range(B):
                x_lo(b)
                if b + 1 < B:
                    coefficients(b + 1)
            for e in range(1, E):
                if e >= 2:
                    pool.wait_ge(y_full, (e - 1) * B * TB)
                for n in range(NPIECES):
                    split_piece(pool, e, n, lambda hi, src: pool.tensor_scalar(hi, src, 1.0, 1.0, ALU.mult, ALU.mult))

        @block.scalar
        def _(act):
            def normalise(b):
                act.wait_ge(coef_done, b + 1)
                if b >= 1:
                    act.wait_ge(ln_full, LN_USES * (b - 1) + 3)
                for i in range(TB):
                    act.activation(xn[:, i, :], X[:, TB * b + i, :], ACT.Identity,
                                   bias=neg_mean_rstd[:, i, :], scale=rstd[:, i, :]).then_inc(xn_done, 1)

            def x_hi(b):
                cols = slice(NB * b, NB * b + NB)
                for c in range(2):
                    act.wait_ge(ln_free, LN_USES * b + c + 1)
                    act.activation(XS[:, c, cols], xt[:, c, :], ACT.Copy).then_inc(xs_hi, 1)
                act.wait_ge(ln_free, LN_USES * b + 3)
                act.activation(XS[0:CR, 4, cols], xt_rest[:, :], ACT.Copy).then_inc(xs_hi, 1)
                act.activation(XS[2 * CR:3 * CR, 4, cols], xt_rest[:, :], ACT.Copy).then_inc(xs_hi, 1)

            def weights_exp(b):
                if E > 1:
                    act.wait_ge(shifted_done, b + 1)
                    act.activation(ex[:, :, :], shifted[:, :, :], ACT.Exp).then_inc(ex_done, 1)

            def gelu(i, e, c):
                n = i * NHC + c
                act.wait_ge(h_full, n + 1)
                if not isinstance(n, int) or n >= 3:
                    act.wait_ge(h_lo, n - 2)
                act.activation(G[:, c % 3, :], ps_h[:, c % 3, :], ACT.Gelu_apprx_tanh,
                               bias=S["b1T"][:, NHC * e + c:NHC * e + c + 1]).then_inc(gelu_done, 1)

            normalise(0)
            x_hi(0)
            for b in range(B):
                weights_exp(b)
                if b + 1 < B:
                    normalise(b + 1)
                for c in range(NHC):
                    gelu(b, 0, c)
                    if c == 2 and b + 1 < B:
                        x_hi(b + 1)
            for e in range(1, E):
                with act.Fori(0, B) as b:
                    for c in range(NHC):
                        gelu(e * B + b, e, c)

        @block.vector
        def _(dve):
            links = [0]

            def link(instruction):
                links[0] += 1
                instruction.then_inc(chain, 1)
                dve.wait_ge(chain, links[0])

            def coefficients(b):
                for i in range(TB):
                    st = dve.bn_stats(stats[:, i, :], X[:, TB * b + i, :])
                st.then_inc(stats_done, 1)
                dve.wait_ge(stats_done, b + 1)
                if b >= 1:
                    dve.wait_ge(coef_done, b)
                for i in range(TB):
                    mv = dve.bn_aggr(mean_var[:, i, :], stats[:, i, :])
                mv.then_inc(mv_done, 1)

            def modulated(b):
                if b >= 1:
                    dve.wait_ge(xs_lo, 2 * b)
                    dve.wait_ge(xs_hi, 4 * b)
                    dve.wait_ge(xs_lo_rest, b)
                for c, rows in enumerate((P, P, CR)):
                    dst = xt_rest[:, :] if c == 2 else xt[:, c, :]
                    dve.wait_ge(ln_full, LN_USES * b + c + 1)
                    dve.tensor_scalar(dst, ps_ln[0:rows, :], modT[0:rows, 3, c, b:b + 1],
                                      modT[0:rows, 2, c, b:b + 1], ALU.mult, ALU.add
                                      ).then_inc(ln_free, 1)
                dve.wait_ge(xs_hi, 4 * b + 4)
                cols = slice(NB * b, NB * b + NB)
                dve.tensor_tensor(XS[CR:2 * CR, 4, cols], xt_rest[:, :], f(XS[0:CR, 4, cols]),
                                  ALU.subtract).then_inc(xs_lo_rest, 1)

            def route(b):
                dve.wait_ge(ln_full, LN_USES * b + 4)
                dve.tensor_copy(logits[:, :, :], ps_ln[:, 0:4 * TB].rearrange("p (t e) -> p t e", e=4)
                                ).then_inc(ln_free, 1)
                dve.wait_ge(ln_free, LN_USES * b + 4)
                pairs = [(lo, hi) for hi in range(4) for lo in range(hi)]
                for n, (lo, hi) in enumerate(pairs):
                    dve.tensor_tensor(beats[:, n, :], logits[:, :, lo], logits[:, :, hi], ALU.is_ge)
                link(dve.reduce_max(best[:, :], logits[:, :, :], AX))
                for e in range(4):
                    start = float(sum(lo == e for lo, _ in pairs))
                    n, (lo, hi) = next((n, p) for n, p in enumerate(pairs) if e in p)
                    sign = -1.0 if lo == e else 1.0
                    step = dve.tensor_scalar(rank[:, :, e], beats[:, n, :], sign, start, ALU.mult, ALU.add)
                link(step)
                for turn in (1, 2):
                    for e in range(4):
                        n, (lo, hi) = [(n, p) for n, p in enumerate(pairs) if e in p][turn]
                        step = dve.tensor_tensor(rank[:, :, e], rank[:, :, e], beats[:, n, :],
                                                 ALU.subtract if lo == e else ALU.add)
                    link(step)
                dve.tensor_tensor(shifted[:, :, :], logits[:, :, :],
                                  best[:, :].unsqueeze(2).to_broadcast([P, TB, 4]), ALU.subtract
                                  ).then_inc(shifted_done, 1)
                dve.wait_ge(ex_done, b + 1)
                link(dve.scalar_tensor_tensor(out=picked[:, :, :], in0=rank[:, :, :], scalar=2.0,
                                              in1=ex[:, :, :], op0=ALU.is_lt, op1=ALU.mult))
                link(dve.reduce_sum(total[:, :], picked[:, :, :], AX))
                link(dve.reciprocal(rtotal[:, :], total[:, :]))
                dve.tensor_tensor(cw[:, TB * b:TB * b + TB, :], picked[:, :, :],
                                  rtotal[:, :].unsqueeze(2).to_broadcast([P, TB, 4]), ALU.mult
                                  ).then_inc(cw_done, 1)
                dve.wait_ge(cw_done, b + 1)

            def split_h(i, c):
                n = i * NHC + c
                dve.wait_ge(gelu_done, n + 1)
                if not isinstance(i, int) or i >= 1 or c >= 3:
                    if c >= 3:
                        dve.wait_ge(h_used, i * 8 + (c - 2))
                    elif c == 2:
                        dve.wait_ge(y_full, i * TB)
                    else:
                        dve.wait_ge(h_used, i * 8 - (1 - c))
                dve.tensor_copy(HHI[:, c % 3, :], G[:, c % 3, :]).then_inc(h_hi, 1)
                dve.wait_ge(h_hi, n + 1)
                dve.tensor_tensor(HLO[:, c % 3, :], G[:, c % 3, :], f(HHI[:, c % 3, :]),
                                  ALU.subtract).then_inc(h_lo, 1)

            def accumulate(i, e, b):
                for k in range(TB):
                    dve.wait_ge(y_full, i * TB + (k + 1))
                    dve.tensor_tensor(y[:, k, :], ps_y[:, k, 0:C], S["b2"][:, e, :], ALU.add
                                      ).then_inc(y_free, 1)
                for k in range(TB):
                    dve.wait_ge(y_free, i * TB + (k + 1))
                    dve.sem_inc(parted, 1)
                    dve.tensor_tensor(y[:, k:k + 1, :], y[:, k:k + 1, :], gates[:, 1, bass.ds(b, 1), :],
                                      ALU.mult).then_inc(y_gated, 1)
                for k in range(TB):
                    dve.wait_ge(y_gated, i * TB + (k + 1))
                    dve.sem_inc(parted, 1)
                    x_tile = X[:, bass.ds(b * TB + k, 1), :]
                    if E > 1:
                        dve.scalar_tensor_tensor(out=x_tile, in0=y[:, k:k + 1, :],
                                                 scalar=cw[:, bass.ds(b * TB + k, 1), e:e + 1],
                                                 in1=x_tile, op0=ALU.mult, op1=ALU.add
                                                 ).then_inc(x_done, 1)
                    else:
                        dve.tensor_tensor(x_tile, x_tile, y[:, k:k + 1, :], ALU.add).then_inc(x_done, 1)

            for n in range(NPIECES):
                if n == 1:
                    coefficients(0)
                if n == 3:
                    modulated(0)
                split_piece(dve, 0, n, lambda hi, src: dve.tensor_copy(hi, src))
            for b in range(B):
                if E > 1:
                    route(b)
                if b + 1 < B:
                    coefficients(b + 1)
                for c in range(NHC):
                    split_h(b, c)
                    if c == 1 and b + 1 < B:
                        modulated(b + 1)
                accumulate(b, 0, b)
            for e in range(1, E):
                with dve.Fori(0, B) as b:
                    for c in range(NHC):
                        split_h(e * B + b, c)
                    accumulate(e * B + b, e, b)

        @block.tensor
        def _(pe):
            def x_transposes(b):
                pe.wait_ge(xn_done, TB * b + TB)
                for c, rows in enumerate((P, P, CR)):
                    n = LN_USES * b + c
                    if n >= 1:
                        pe.wait_ge(ln_free, n)
                    for i in range(TB):
                        mm = pe.transpose(ps_ln[0:rows, P * i:P * i + P],
                                          xn[:, i, P * c:P * c + rows], ident[:, :])
                    mm.then_inc(ln_full, 1)

            def stack_ready(b):
                pe.wait_ge(xs_hi, 4 * b + 4)
                pe.wait_ge(xs_lo, 2 * b + 2)
                pe.wait_ge(xs_lo_rest, b + 1)

            def route_logits(b):
                if E > 1:
                    pe.wait_ge(ln_free, LN_USES * b + 3)
                    for i in range(TB):
                        at = P * (TB * b + i)
                        for n, (w, x) in enumerate(PAIRS):
                            r = rows_of(w)
                            mm = pe.matmul(ps_ln[:, 4 * i:4 * i + 4], XS[0:r, x, at:at + P],
                                           S["Wgate"][0:r, w, :], start=(n == 0),
                                           stop=(n == len(PAIRS) - 1))
                    mm.then_inc(ln_full, 1)

            def up(i, e, b, c):
                n = i * NHC + c
                if not isinstance(n, int) or n >= 3:
                    pe.wait_ge(gelu_done, n - 2)
                for m, (w, x) in enumerate(PAIRS):
                    r = rows_of(w)
                    mm = pe.matmul(ps_h[:, c % 3, :], W1[e % n_slots][0:r, w, P * c:P * c + P],
                                   XS[0:r, x, bass.ds(b * NB, NB)], start=(m == 0),
                                   stop=(m == len(PAIRS) - 1))
                mm.then_inc(h_full, 1)

            def down(i, e, c):
                if c == 0 and (not isinstance(i, int) or i >= 1):
                    pe.wait_ge(y_free, i * TB)
                pe.wait_ge(h_lo, i * NHC + (c + 1))
                w2 = W2[e % n_slots]
                for k in range(TB):
                    cols = slice(P * k, P * k + P)
                    for m, (h, w) in enumerate(((HHI, 0), (HHI, 1), (HLO, 0))):
                        mm = pe.matmul(ps_y[:, k, 0:C], h[:, c % 3, cols], w2[:, w, c, :],
                                       start=(c == 0 and m == 0), stop=(c == NHC - 1 and m == 2))
                    if c == NHC - 1:
                        mm.then_inc(y_full, 1)
                if c < NHC - 1:
                    mm.then_inc(h_used, 1)

            def expert(i, e, b, between=None):
                for c in range(NHC):
                    up(i, e, b, c)
                    if c >= 2:
                        down(i, e, c - 2)
                    if between is not None and c in between:
                        between[c]()
                down(i, e, NHC - 2)
                down(i, e, NHC - 1)

            x_transposes(0)
            stack_ready(0)
            route_logits(0)
            pe.wait_ge(split_done, NPIECES)
            for b in range(B):
                if b + 1 < B:
                    expert(b, 0, b, {1: lambda: x_transposes(b + 1)})
                    stack_ready(b + 1)
                    route_logits(b + 1)
                else:
                    expert(b, 0, b)
            for e in range(1, E):
                pe.wait_ge(split_done, (e + 1) * NPIECES)
                with pe.Fori(0, B) as b:
                    expert(e * B + b, e, b)


def build(nc, A, out):
    outer = ExitStack()
    with outer:
        layer_sems = []

        def sem(name):
            layer_sems.append(nc.alloc_semaphore(name=name))
            return layer_sems[-1]

        def sb(ctx, name, shape, dt):
            return ctx.enter_context(nc.sbuf_tensor(name, shape, dt))

        def pb(ctx, name, shape, dt):
            return ctx.enter_context(nc.psum_tensor(name, shape, dt))

        S = {name: sb(outer, name, shape, dt) for name, shape, dt in (
            ("X", [P, T, C], F32),
            ("ident", [P, P], F32),
            ("neg_half", [P, 2 * NH], F32),
            ("condT", [P, 3, B], F32),
            ("modT", [P, 4, 3, B], F32),
            ("gates", [P, 2, B, C], F32),
            ("b1T", [P, 4 * NHC], F32),
            ("b2", [P, 4, C], F32),
            ("Wgate", [P, 5, 4], F32R),
        )}
        for l, p in enumerate(("L0_cond_", "L1_cond_")):
            one = l == 0
            L = {"l": l, "E": 1 if one else 4, "x": A["x"], "cond": A["cond_1152"],
                 "out": None if one else out}
            for name in ("w_qkv", "b_qkv", "w_proj", "b_proj"):
                L[name] = A[p + name]
            L["w_mod"], L["b_mod"] = ((A[p + "w_mod"], A[p + "b_mod"]) if one
                                      else (A[p + "w_adaln"], A[p + "b_adaln"]))
            if one:
                L["g_q"], L["g_k"] = A[p + "g_q"], A[p + "g_k"]
                for name in ("w1", "w2"):
                    L[name] = A[p + name].unsqueeze(0)
                for name in ("b1", "b2"):
                    L[name] = A[p + name].unsqueeze(0)
            else:
                for name in ("w1", "w2", "b1", "b2", "w_gate"):
                    L[name] = A[p + name]
            attn = ExitStack()
            with attn:
                for name, shape, dt in (("Wqkv", [P, 5, 3 * C], F32R), ("Wproj", [P, 5, C], F32R),
                                        ("bqkv", [P, 3 * C], F32), ("bproj", [P, C], F32),
                                        ("gain", [P, 2, HD], F32)):
                    S[name] = sb(attn, f"{name}{l}", shape, dt)
                setup(nc, sem, sb, pb, L, S, one)
                attention(nc, sem, sb, pb, L, S)
            mlp(nc, sem, sb, pb, L, S)
            if one:
                nc.clear_and_free_semaphores(layer_sems)
                nc.all_engine_barrier()
                layer_sems = []


_INS = ['x', 'cond_1152', 'L0_cond_w_mod', 'L0_cond_b_mod', 'L0_cond_w_qkv', 'L0_cond_b_qkv',
        'L0_cond_g_q', 'L0_cond_g_k', 'L0_cond_w_proj', 'L0_cond_b_proj', 'L0_cond_w1', 'L0_cond_b1',
        'L0_cond_w2', 'L0_cond_b2', 'L1_cond_w_adaln', 'L1_cond_b_adaln', 'L1_cond_w_qkv',
        'L1_cond_b_qkv', 'L1_cond_w_proj', 'L1_cond_b_proj', 'L1_cond_w_gate', 'L1_cond_w1',
        'L1_cond_b1', 'L1_cond_w2', 'L1_cond_b2']


def kernel(**inputs):
    import numpy as _np
    import concourse.bacc as _bacc
    from concourse import mybir as _mybir
    from concourse.bass_utils import run_bass_kernel_spmd as _run

    nc = _bacc.Bacc("TRN2", target_bir_lowering=False, num_devices=1)
    arrays, args = {}, {}
    for name in _INS:
        a = _np.ascontiguousarray(inputs[name])
        arrays[f"in_{name}"] = a
        args[name] = nc.dram_tensor(f"in_{name}", a.shape, _mybir.dt.from_np(a.dtype),
                                    kind="ExternalInput").ap()
    out = nc.dram_tensor("out_0", (B, NB, C), F32, kind="ExternalOutput").ap()
    build(nc, args, out)
    r = _run(nc, [arrays], core_ids=[0])
    return r.results[0]["out_0"]
```

```python
from contextlib import ExitStack

import concourse.bass as bass
from concourse import mybir

F32 = mybir.dt.float32
F32R = mybir.dt.float32r
ALU = mybir.AluOpType
ACT = mybir.ActivationFunctionType
AX = mybir.AxisListType.X

P = 128
B = 4
NB = 512
TB = NB // P
T = B * TB
C = 288
CR = C - 2 * P
NH = 16
HD = C // NH
HG = 4
NG = NH // HG
GC = HG * HD
HID = 4 * C
NHC = HID // P
QKW = 2 * C
HALF = 3 * C // 2
EPS = 1e-6
KS_ROWS = 96
M_ROW = 3 * HD


def f(ap):
    return ap.bitcast(F32)


PAIRS = [(0, 0), (1, 1), (0, 2), (1, 3), (2, 0), (3, 1), (4, 4)]


def rows_of(plane):
    return 96 if plane == 4 else P


class BankOrder:

    BODY = (["xA", "xB", "xC", "q3", "k3", "qkv0a", "qkv0b", "qkv1a", "qkv1b"]
            + ["qkv2a", "qkv2b", "qkv3a", "qkv3b", "oA", "oB", "oC", "o0", "proj0", "proj1", "o1"]
            + ["q0", "k0", "proj2", "proj3", "o2", "q1", "k1", "q2", "k2", "o3"])
    OUTPUT = ["oA", "oB", "oC", "proj0", "proj1", "proj2", "proj3"]
    PREPARED = [u for u in BODY if u[0] in "xqk" and u not in ("q3", "k3")]

    def __init__(self):
        rounds = B - 2
        self.uses, self.start, n = {}, {}, 0
        for section, uses, times in (
                ("before", self.PREPARED, 1),
                ("first", [u for u in self.BODY if u not in self.OUTPUT], 1),
                ("loop", self.BODY, rounds),
                ("last", [u for u in self.BODY if u not in self.PREPARED], 1),
                ("after", self.OUTPUT, 1)):
            self.uses[section], self.start[section] = uses, n
            n += len(uses) * times

    def at(self, use, where):
        section, b = where
        n = self.start[section] + self.uses[section].index(use)
        turn = n // 2 + 1
        if section == "loop":
            turn = b * (len(self.BODY) // 2) + (turn - len(self.BODY) // 2)
        return n % 2, turn


ORDER = BankOrder()


def split_weights(eng, copy, split_step, n0, stack, raw, raw_rest):
    copy(stack[:, 0:2, :], raw)
    copy(stack[0:96, 4, :], raw_rest).then_inc(split_step, 1)
    eng.wait_ge(split_step, n0 + 1)
    eng.tensor_tensor(stack[:, 2:4, :], raw, f(stack[:, 0:2, :]), ALU.subtract).then_inc(split_step, 1)
    eng.wait_ge(split_step, n0 + 2)
    eng.tensor_tensor(stack[64:96, 4, :], raw_rest[64:96, :], f(stack[64:96, 4, :]),
                      ALU.subtract).then_inc(split_step, 1)
    eng.wait_ge(split_step, n0 + 3)


def refine_root(dve, link, r, v, scratch):
    link(dve.tensor_tensor(scratch, r, r, ALU.mult))
    link(dve.tensor_tensor(scratch, scratch, v, ALU.mult))
    link(dve.tensor_scalar(scratch, scratch, -0.5, 1.5, ALU.mult, ALU.add))
    return dve.tensor_tensor(r, r, scratch, ALU.mult)


class AttentionWeights:

    def __init__(self, ctx, sem, sb, L, S):
        l = L["l"]
        self.loads = []
        self.tiles = []
        for name, cols, dst in (("w_qkv", 3 * C, S["Wqkv"]), ("w_proj", C, S["Wproj"]),
                                ("w_gate", 4, S["Wgate"])):
            if name in L:
                raw = sb(ctx, f"raw_{name}{l}", [P, 2, cols], F32)
                rest = sb(ctx, f"raw_{name}_rest{l}", [96, cols], F32)
                self.tiles.append((dst, raw, rest))
                self.loads.append((raw[:, :, :], L[name][0:2 * P, :].rearrange("(k p) n -> p k n", p=P)))
                for r in range(3):
                    self.loads.append((rest[CR * r:CR * r + CR, :], L[name][2 * P:C, :]))
        self.biases = [(S["bqkv"][:, :], L["b_qkv"].partition_broadcast(P)),
                       (S["bproj"][:, :], L["b_proj"].partition_broadcast(P))]
        if l == 0:
            self.biases += [(S["gain"][:, i, :], g.partition_broadcast(P))
                            for i, g in enumerate((L["g_q"], L["g_k"]))]
        self.weights_in = sem(f"weights_in{l}")
        self.biases_in = sem(f"biases_in{l}")
        self.split_step = sem(f"split_step{l}")

    def load(self, queue):
        for dst, src in self.loads:
            queue.dma_start(dst, src).then_inc(self.weights_in, 16)
        for dst, src in self.biases:
            queue.dma_start(dst, src).then_inc(self.biases_in, 16)

    def split(self, eng, copy):
        eng.wait_ge(self.weights_in, 16 * len(self.loads))
        for n, (dst, raw, rest) in enumerate(self.tiles):
            split_weights(eng, copy, self.split_step, 3 * n, dst, raw[:, :, :], rest[:, :])

    def wait_biases(self, queue):
        queue.wait_ge(self.biases_in, 16 * len(self.biases))


def setup(nc, sem, sb, pb, layers, S):
    ctx = ExitStack()
    with ctx:
        def t(name, shape, dt=F32):
            return sb(ctx, f"{name}_s", shape, dt)

        wm = [t(f"wm{l}", [P, 2, 6 * C]) for l in range(2)]
        wm_rest = [t(f"wm_rest{l}", [CR + 1, 6 * C]) for l in range(2)]
        cond = t("cond", [B, C])
        cond_silu = t("cond_silu", [B, C])
        condT = t("condT", [P, 3, B])
        mod = [t(f"mod{l}", [B, 6 * C]) for l in range(2)]
        b1_rows = [t(f"b1_rows{l}", [L["E"] * NHC, P]) for l, L in enumerate(layers)]
        ps_mod = pb(ctx, "ps_mod_s", [P, 4, 512], F32)
        ps_small = pb(ctx, "ps_small_s", [P, 4, 512], F32)
        weights = AttentionWeights(ctx, sem, sb, layers[0], S)

        cond_in = sem("cond_in")
        mod_in = [sem(f"mod_in{l}") for l in range(2)]
        rows_in = sem("rows_in")
        x_in = sem("x_in")
        ident_step = sem("ident_step")
        rows_zero = sem("rows_zero")
        silu_done = sem("silu_done")
        ct_ones = sem("ct_ones")
        ct_ps = sem("ct_ps")
        ct_done = sem("ct_done")
        mod_ps = sem("mod_ps")
        mod_done = sem("mod_done")
        modt_ps = sem("modt_ps")
        mod_out = sem("mod_out")

        block = ctx.enter_context(nc.Block())

        @block.sync
        def _(sp):
            sp.dma_start(cond[:, :], layers[0]["cond"]).then_inc(cond_in, 16)
            for l, L in enumerate(layers):
                sp.dma_start(wm[l][:, :, :], L["w_mod"][0:2 * P, :].rearrange("(k p) n -> p k n", p=P)
                             ).then_inc(mod_in[l], 16)
                sp.dma_start(wm_rest[l][0:CR, :], L["w_mod"][2 * P:C, :]).then_inc(mod_in[l], 16)
                sp.dma_start(wm_rest[l][CR:CR + 1, :], L["b_mod"].rearrange("(a n) -> a n", a=1)
                             ).then_inc(mod_in[l], 16)
                sp.dma_start(b1_rows[l][:, :], L["b1"].rearrange("e (k p) -> (e k) p", p=P)
                             ).then_inc(rows_in, 16)
            weights.load(sp)
            sp.dma_start(S["X"][:, :, :], layers[0]["x"].rearrange("b (t p) c -> p (b t) c", p=P)
                         ).then_inc(x_in, 16)
            for l in range(2):
                sp.wait_ge(mod_done, 4 * l + 4)
                sp.dma_start(S["mod_rows"][l], mod[l][:, :]).then_inc(mod_out, 16)
            sp.wait_ge(mod_out, 32)
            weights.wait_biases(sp)
            sp.wait_ge(x_in, 16)

        @block.gpsimd
        def _(pool):
            pool.memset(S["neg_half"][:, :], -0.5)
            pool.memset(S["ident"][:, :], 0.0).then_inc(ident_step, 1)
            pool.wait_ge(ident_step, 1)
            pool.affine_select(out=S["ident"][:, :], in_=S["ident"][:, :], compare_op=ALU.not_equal,
                               fill=1.0, base=0, pattern=[[-1, P]], channel_multiplier=1
                               ).then_inc(ident_step, 1)
            pool.wait_ge(ident_step, 2)
            pool.memset(condT[CR:CR + 1, 2, :], 1.0).then_inc(ct_ones, 1)
            pool.wait_ge(ct_ones, 1)
            clear_stacks(pool, S, rows_zero)

        @block.scalar
        def _(act):
            act.wait_ge(cond_in, 16)
            act.activation(cond_silu[:, :], cond[:, :], ACT.Silu).then_inc(silu_done, 1)
            for n in range(8):
                act.wait_ge(mod_ps, n + 1)
                cols = slice(HALF * (n % 4), HALF * (n % 4) + HALF)
                act.activation(mod[n // 4][:, cols], ps_mod[0:B, n % 4, 0:HALF], ACT.Copy
                               ).then_inc(mod_done, 1)

        @block.vector
        def _(dve):
            dve.wait_ge(ct_ps, 1)
            dve.tensor_copy(condT[:, 0:2, :], ps_small[:, 0, 0:8].rearrange("p (k b) -> p k b", k=2))
            dve.tensor_copy(condT[0:CR, 2, :], ps_small[0:CR, 0, 8:12]).then_inc(ct_done, 1)
            weights.split(dve, dve.tensor_copy)
            for l, L in enumerate(layers):
                dve.wait_ge(modt_ps, l + 1)
                for v in range(4):
                    for k, rows in ((0, P), (1, P), (2, CR)):
                        src = ps_small[0:rows, 2 * l, 16 + (3 * v + k) * 4:16 + (3 * v + k) * 4 + 4]
                        dst = S["modT"][l][0:rows, v, k, :]
                        if v % 2:
                            dve.tensor_scalar(dst, src, 1.0, None, ALU.add)
                        else:
                            dve.tensor_copy(dst, src)
                n_rows = L["E"] * NHC
                dve.tensor_copy(S["b1T"][l][:, 0:n_rows], ps_small[:, 2 * l + 1, 0:n_rows])

        @block.tensor
        def _(pe):
            ident = S["ident"]
            pe.wait_ge(ident_step, 2)
            pe.wait_ge(silu_done, 1)
            for k, rows in ((0, P), (1, P), (2, CR)):
                mm = pe.transpose(ps_small[0:rows, 0, 4 * k:4 * k + 4],
                                  cond_silu[:, P * k:P * k + rows], ident[0:B, 0:B])
            mm.then_inc(ct_ps, 1)
            pe.wait_ge(ct_done, 1)
            pe.wait_ge(ct_ones, 1)
            for l, L in enumerate(layers):
                pe.wait_ge(mod_in[l], 48)
                for n in range(4):
                    if l > 0:
                        pe.wait_ge(mod_done, n + 1)
                    cols = slice(HALF * n, HALF * n + HALF)
                    for k in range(2):
                        pe.matmul(ps_mod[0:B, n, 0:HALF], condT[:, k, :], wm[l][:, k, cols],
                                  start=(k == 0), stop=False)
                    pe.matmul(ps_mod[0:B, n, 0:HALF], condT[0:CR + 1, 2, :], wm_rest[l][:, cols],
                              start=False, stop=True).then_inc(mod_ps, 1)
                pe.wait_ge(mod_done, 4 * l + 4)
                for v, part in enumerate((0, 1, 3, 4)):
                    for k, rows in ((0, P), (1, P), (2, CR)):
                        at = 16 + (3 * v + k) * 4
                        pe.transpose(ps_small[0:rows, 2 * l, at:at + 4],
                                     mod[l][:, C * part + P * k:C * part + P * k + rows],
                                     ident[0:B, 0:B])
                pe.wait_ge(rows_in, 32)
                n_rows = L["E"] * NHC
                pe.transpose(ps_small[:, 2 * l + 1, 0:n_rows], b1_rows[l][:, :],
                             ident[0:n_rows, 0:n_rows]).then_inc(modt_ps, 1)


def clear_stacks(pool, S, rows_zero):
    pool.memset(f(S["zero_row"][:, :]), 0.0).then_inc(rows_zero, 1)
    pool.wait_ge(rows_zero, 1)
    for g in range(NG):
        pool.memset(f(S[f"STK{g}"][:, 0, :, :]), 0.0)
        pool.memset(f(S[f"STK{g}"][:, 1, :, :]), 1.0).then_inc(rows_zero, 1)


def attention(nc, sem, sb, pb, L, S):
    l = L["l"]
    head_norm = l == 0
    X, ident = S["X"], S["ident"]
    Wqkv, Wproj, modT, gates = S["Wqkv"], S["Wproj"], S["modT"][l], S["gates"]
    SCALE = float(HD) ** -0.5
    QK0 = 2 if head_norm else 1
    ctx = ExitStack()
    with ctx:
        def t(name, shape, dt=F32):
            return sb(ctx, f"{name}_a{l}", shape, dt)

        stats = t("stats", [P, T, 6])
        mean_var = t("mean_var", [P, T, 2])
        var_eps = t("var_eps", [P, T, 1])
        neg_mean = t("neg_mean", [P, T, 1])
        rstd = t("rstd", [P, T, 1])
        neg_mean_rstd = t("neg_mean_rstd", [P, T, 1])
        xn = t("xn", [P, TB, C])
        y = xn
        xt = t("xt", [P, 2, NB])
        xt_rest = t("xt_rest", [CR, NB])
        XS = t("XS", [P, 5, NB], F32R)
        qk = t("qk", [P, 2, QKW])
        qk_sq = t("qk_sq", [P, QKW])
        h_sum = t("h_sum", [P, 2 * NH])
        h_mean = t("h_mean", [P, TB, 2 * NH])
        h_var = t("h_var", [P, TB, 2 * NH])
        h_ve = t("h_ve", [P, 2 * NH])
        h_v = t("h_v", [P, 2 * NH])
        h_rstd = t("h_rstd", [P, 2 * NH])
        QKN = t("QKN", [P, TB, 2 * NG, HD, HG])
        v_in = t("v_in", [P, TB, C])
        V = t("V", [P, TB, NH, HD + 1])
        src = t("src", [GC, 4, NB], F32R)
        zero_row = S["zero_row"]
        STK = [S[f"STK{g}"] for g in range(NG)]
        neg_max = t("neg_max", [P, HG * TB])
        neg_max_rows = t("neg_max_rows", [HG * TB, P], F32R)
        probs = t("probs", [P, 2, HG, NB])
        OT = t("OT", [P, NB])
        rden = t("rden", [P, NG, TB, HG])
        ON = t("ON", [P, TB, C])

        MAX_RING, RING = 3, 2
        ps_shared = pb(ctx, f"ps_shared{l}", [P, 2, 512], F32)
        ps_max = pb(ctx, f"ps_max{l}", [P, MAX_RING, 512], F32)
        ps_ring = pb(ctx, f"ps_ring{l}", [P, RING, 512], F32)
        ps_out = pb(ctx, f"ps_out{l}", [P, 512], F32)

        def s(name):
            return sem(f"{name}_a{l}")

        parted = s("parted")
        rows_zero = s("rows_zero")
        late_in = s("late_in")
        inited = s("inited")
        stats_done = s("stats_done")
        mv_done = s("mv_done")
        chain = s("chain")
        root_done = s("root_done")
        ve_done = s("ve_done")
        rstd_done = s("rstd_done")
        coef_done = s("coef_done")
        xn_done = s("xn_done")
        xs_hi = s("xs_hi")
        xs_lo = s("xs_lo")
        xs_lo_rest = s("xs_lo_rest")
        full = [s("full0"), s("full1")]
        free = [s("free0"), s("free1")]
        qk_done = s("qk_done")
        h_sum_done = s("h_sum_done")
        h_mean_done = s("h_mean_done")
        cen_done = s("cen_done")
        sq_done = s("sq_done")
        h_var_done = s("h_var_done")
        h_v_done = s("h_v_done")
        h_rstd_done = s("h_rstd_done")
        cen_scaled = s("cen_scaled")
        qkn_done = s("qkn_done")
        v_ones = s("v_ones")
        v_done = s("v_done")
        hi_done = s("hi_done")
        loaded = [s(f"loaded{g}") for g in range(NG)]
        max_full = s("max_full")
        max_done = s("max_done")
        m_loaded = s("m_loaded")
        ring_full = s("ring_full")
        ring_done = s("ring_done")
        pv_done = s("pv_done")
        ot_done = s("ot_done")
        rden_done = s("rden_done")
        o_hi = s("o_hi")
        last_gated = s("last_gated")
        y_gated = s("y_gated")
        x_done = s("x_done")

        Q_LO, Q_HI, K_HI, K_LO = range(4)
        PARTS = [(Q_HI, K_HI), (Q_LO, K_HI), (Q_HI, K_LO)]
        HI_OF, LO_OF = {"q": Q_HI, "k": K_HI}, {"q": Q_LO, "k": K_LO}
        LATE = 16 * (2 + L["E"])
        FIRST_LOADS = 16 * 2 * len(PARTS)
        LOADS = 16 * (2 * len(PARTS) + 1)

        SCORES = HG * TB
        EVENTS = SCORES + 1

        def events(b, g):
            return b * (NG * EVENTS) + (EVENTS * g + 1)

        block = ctx.enter_context(nc.Block())

        @block.tensor
        def _(pe):
            def fill(use, where):
                k, n = ORDER.at(use, where)
                if not isinstance(n, int) or n > 1:
                    pe.wait_ge(free[k], n - 1)
                return ps_shared[:, k, :], full[k]

            def transposes(use, where, rows, tile):
                ps, filled = fill(use, where)
                for i in range(TB):
                    mm = pe.transpose(ps[0:rows, P * i:P * i + P], tile(i), ident[:, :])
                mm.then_inc(filled, 1)

            def x_transposes(where, nb, uses):
                pe.wait_ge(xn_done, nb * TB + TB)
                for c, (use, rows) in enumerate((("xA", P), ("xB", P), ("xC", CR))):
                    if use in uses:
                        transposes(use, where, rows, lambda i: xn[:, i, P * c:P * c + rows])

            def o_transposes(where):
                for c, (use, rows) in enumerate((("oA", P), ("oB", P), ("oC", CR))):
                    transposes(use, where, rows, lambda i: ON[:, i, P * c:P * c + rows])

            def qk_transposes(where, g):
                for s_, name in enumerate("qk"):
                    transposes(f"{name}{g}", where, GC,
                               lambda i: QKN[:, i, NG * s_ + g, :, :].rearrange("p d j -> p (d j)"))

            def out_transposes(where, b, g):
                pe.wait_ge(ot_done, b * NG + (g + 1))
                transposes(f"o{g}", where, P, lambda i: OT[:, P * i:P * i + P])

            def qkv(where, nb, i):
                if i == 0:
                    pe.wait_ge(xs_hi, nb * 4 + 4)
                    pe.wait_ge(xs_lo, nb * 2 + 2)
                    pe.wait_ge(xs_lo_rest, nb + 1)
                for h in range(2):
                    ps, filled = fill(f"qkv{i}{'ab'[h]}", where)
                    for n, (w, x) in enumerate(PAIRS):
                        r = rows_of(w)
                        mm = pe.matmul(ps[:, 0:HALF], XS[0:r, x, P * i:P * i + P],
                                       Wqkv[0:r, w, HALF * h:HALF * h + HALF],
                                       start=(n == 0), stop=(n == len(PAIRS) - 1))
                    mm.then_inc(filled, 1)

            def project(where, tiles):
                for use in ("oA", "oB", "oC"):
                    k, n = ORDER.at(use, where)
                    pe.wait_ge(free[k], n)
                for i in tiles:
                    ps, filled = fill(f"proj{i}", where)
                    for n, (w, x) in enumerate(PAIRS):
                        r = rows_of(w)
                        mm = pe.matmul(ps[:, 0:C], XS[0:r, x, P * i:P * i + P], Wproj[0:r, w, :],
                                       start=(n == 0), stop=(n == len(PAIRS) - 1))
                    mm.then_inc(filled, 1)

            def max_scores(g, j, i):
                pe.matmul(ps_max[:, (i * HG + j) % MAX_RING, :], STK[g][:, 0, j, P * i:P * i + P],
                          STK[g][:, 1, j, :], start=True, stop=True).then_inc(max_full, 1)

            def exp_scores(b, g, n):
                i, j = divmod(n, HG)
                if n >= RING:
                    pe.wait_ge(ring_done, events(b, g) + (n - RING + 1))
                elif n == 0:
                    pe.wait_ge(ring_done, events(b, g))
                pe.matmul(ps_ring[:, n % RING, :], STK[g][:, 1, j, P * i:P * i + P],
                          STK[g][:, 0, j, :], start=True, stop=True).then_inc(ring_full, 1)

            def max_rows(n_groups, before):
                pe.wait_ge(max_done, n_groups * SCORES)
                if before is not None:
                    pe.wait_ge(ring_done, before)
                pe.transpose(ps_ring[0:SCORES, SCORES % RING, 0:P], neg_max[:, :], ident[:, :]
                             ).then_inc(ring_full, 1)

            def values(b, g, i):
                for j in range(HG):
                    pe.wait_ge(ring_done, events(b, g) + (HG * i + j + 1))
                    mm = pe.matmul(ps_out[32 * j:32 * j + HD + 1, :], V[:, i, HG * g + j, :],
                                   probs[:, i % 2, j, :], start=(i == 0), stop=(i == TB - 1))
                mm.then_inc(pv_done, 1)

            def batch(section, b):
                where, nb = (section, b), b + 1
                prepares, projects = section != "last", section != "first"
                for g in range(NG):
                    ahead = (g + 1) % NG
                    has_ahead = g < NG - 1 or prepares
                    pe.wait_ge(m_loaded, b * (16 * NG) + (16 * g + 16))
                    for i in range(TB):
                        for j in range(HG):
                            n = HG * i + j
                            exp_scores(b, g, n)
                            if has_ahead:
                                if n == 0:
                                    pe.wait_ge(loaded[ahead],
                                               (nb if ahead == 0 else b) * LOADS + FIRST_LOADS)
                                if n >= MAX_RING:
                                    pe.wait_ge(max_done, b * (NG * SCORES)
                                               + (SCORES * (g + 1) + n - MAX_RING + 1))
                                max_scores(ahead, j, i)
                            if j == 1 and i >= 1:
                                if (g, i) == (0, 1):
                                    pe.wait_ge(v_done, b + 1)
                                values(b, g, i - 1)
                        if prepares and (g, i) == (0, 0):
                            x_transposes(where, nb, ("xA", "xB"))
                        if prepares and (g, i) == (0, 1):
                            x_transposes(where, nb, ("xC",))
                        if (g, i) == (0, 2):
                            qk_transposes(where, NG - 1)
                        if prepares and (g, i) in ((0, 3), (1, 0), (1, 1)):
                            qkv(where, nb, {(0, 3): 0, (1, 0): 2, (1, 1): 3}[g, i])
                        if projects and (g, i) == (1, 2):
                            o_transposes(where)
                        if (g, i) == (1, 3):
                            out_transposes(where, b, 0)
                        if prepares and (g, i) == (2, QK0):
                            pe.wait_ge(qkn_done, nb * TB + TB)
                            qk_transposes(where, 0)
                        if prepares and (g, i) == (3, 1):
                            qk_transposes(where, 1)
                    if has_ahead:
                        max_rows(b * NG + (g + 2), events(b, g) + (SCORES - RING + 1))
                    values(b, g, TB - 1)
                    if g == 0:
                        if prepares:
                            qkv(where, nb, 1)
                        pe.wait_ge(ot_done, b * NG + 1)
                    else:
                        if projects and g < NG - 1:
                            project(where, (2 * g - 2, 2 * g - 1))
                        if prepares and g == NG - 1:
                            qk_transposes(where, 2)
                        out_transposes(where, b, g)

            before, after = ("before", None), ("after", None)
            x_transposes(before, 0, ("xA", "xB", "xC"))
            for i in range(TB):
                qkv(before, 0, i)
            pe.wait_ge(qkn_done, TB)
            for g in range(NG - 1):
                qk_transposes(before, g)
            pe.wait_ge(inited, 1)
            pe.wait_ge(loaded[0], FIRST_LOADS)
            for i in range(TB):
                for j in range(HG):
                    if i * HG + j >= MAX_RING:
                        pe.wait_ge(max_done, i * HG + j - MAX_RING + 1)
                    max_scores(0, j, i)
            max_rows(1, None)
            batch("first", 0)
            with pe.Fori(1, B - 1) as b:
                batch("loop", b)
            batch("last", B - 1)
            k, n = ORDER.at(f"o{NG - 1}", ("last", B - 1))
            pe.wait_ge(free[k], n)
            o_transposes(after)
            project(after, range(TB))

        @block.scalar
        def _(act):
            def normalise(nb):
                if isinstance(nb, int) and nb <= 1:
                    act.wait_ge(coef_done, nb + 1)
                if isinstance(nb, int) and nb == 1:
                    k, n = ORDER.at("xC", ("before", None))
                    act.wait_ge(full[k], n)
                elif not isinstance(nb, int):
                    act.wait_ge(x_done, nb - 1)
                    act.sem_inc(parted, 1)
                for i in range(TB):
                    one = bass.ds(nb * TB + i, 1)
                    act.activation(xn[:, i:i + 1, :], X[:, one, :], ACT.Identity,
                                   bias=neg_mean_rstd[:, one, :], scale=rstd[:, one, :]
                                   ).then_inc(xn_done, 1)

            def x_hi(where):
                for c, use in enumerate(("xA", "xB")):
                    k, n = ORDER.at(use, where)
                    act.wait_ge(free[k], n)
                    act.activation(XS[:, c, :], xt[:, c, :], ACT.Copy).then_inc(xs_hi, 1)
                k, n = ORDER.at("xC", where)
                act.wait_ge(free[k], n)
                act.activation(XS[0:CR, 4, :], xt_rest[:, :], ACT.Copy).then_inc(xs_hi, 1)
                act.activation(XS[2 * CR:3 * CR, 4, :], xt_rest[:, :], ACT.Copy).then_inc(xs_hi, 1)

            def squares(nb, i):
                if head_norm:
                    if not (isinstance(nb, int) and nb == 0 and i == 0):
                        act.wait_ge(h_var_done, nb * TB + i)
                    act.wait_ge(cen_done, nb * TB + (i + 1))
                    act.activation(qk_sq[:, :].rearrange("p (g j d) -> p g d j", j=HG, d=HD),
                                   QKN[:, i, :, :, :], ACT.Square).then_inc(sq_done, 1)

            def qk_hi(where, nb, g):
                first = isinstance(nb, int) and nb == 0
                if g >= 1:
                    act.wait_ge(loaded[g - 1], nb * LOADS + FIRST_LOADS)
                elif not first:
                    act.wait_ge(loaded[NG - 1], (nb - 1) * LOADS + FIRST_LOADS)
                for name in "qk":
                    k, n = ORDER.at(f"{name}{g}", where)
                    act.wait_ge(full[k], n)
                    act.activation(src[:, HI_OF[name], :], ps_shared[0:GC, k, :], ACT.Copy
                                   ).then_inc(hi_done, 1)

            def max_rows(event, n_groups):
                if not isinstance(n_groups, int) or n_groups >= 1:
                    act.wait_ge(m_loaded, n_groups * 16)
                act.wait_ge(ring_full, event + 1)
                act.activation(neg_max_rows[:, :], ps_ring[0:SCORES, SCORES % RING, 0:P], ACT.Copy
                               ).then_inc(ring_done, 1)

            def o_hi_parts(where):
                for c, (use, rows) in enumerate((("oA", P), ("oB", P), ("oC", CR))):
                    k, n = ORDER.at(use, where)
                    act.wait_ge(full[k], n)
                    if c < 2:
                        act.activation(XS[:, c, :], ps_shared[:, k, :], ACT.Copy).then_inc(o_hi, 1)
                    else:
                        for at in (0, 2 * CR):
                            act.activation(XS[at:at + CR, 4, :], ps_shared[0:CR, k, :], ACT.Copy
                                           ).then_inc(o_hi, 1)

            def batch(section, b):
                where, nb = (section, b), b + 1
                prepares, projects = section != "last", section != "first"
                if prepares:
                    normalise(nb)
                for g in range(NG):
                    for i in range(TB):
                        if i >= 2:
                            act.wait_ge(pv_done, b * (NG * TB) + (TB * g + i - 1))
                        for j in range(HG):
                            n = HG * i + j
                            act.wait_ge(ring_full, events(b, g) + (n + 1))
                            act.activation(probs[:, i % 2, j, :], ps_ring[:, n % RING, :], ACT.Exp,
                                           scale=SCALE).then_inc(ring_done, 1)
                        if prepares and (g, i) == (0, 1):
                            x_hi(where)
                        if (g, i) == (0, 2):
                            qk_hi(where, b, NG - 1)
                        if prepares and (g, i) == (1, 0):
                            squares(nb, 1)
                        if projects and (g, i) == (1, 2):
                            o_hi_parts(where)
                        if prepares and (g, i) in ((1, 2), (1, 3)):
                            squares(nb, i)
                        if prepares and (g, i) == (2, QK0):
                            qk_hi(where, nb, 0)
                        if prepares and (g, i) == (3, 1):
                            qk_hi(where, nb, 1)
                    if g < NG - 1 or prepares:
                        max_rows(events(b, g) + SCORES, b * NG + (g + 1))
                    act.wait_ge(pv_done, b * (NG * TB) + (TB * g + TB))
                    act.activation(OT[:, :], ps_out[:, :], ACT.Copy).then_inc(ot_done, 1)
                    if g == 0 and prepares:
                        squares(nb, 0)
                    if g == NG - 1 and prepares:
                        qk_hi(where, nb, 2)

            before = ("before", None)
            act.wait_ge(ve_done, 1)
            act.activation(rstd[:, 0:TB, :], neg_mean[:, 0:TB, :], ACT.Sqrt).then_inc(root_done, 1)
            normalise(0)
            x_hi(before)
            for i in range(TB):
                squares(0, i)
                if head_norm:
                    if i >= 1:
                        act.wait_ge(cen_scaled, i)
                    act.wait_ge(h_v_done, i + 1)
                    act.activation(h_rstd[:, :], h_v[:, :], ACT.Sqrt).then_inc(root_done, 1)
            qk_hi(before, 0, 0)
            qk_hi(before, 0, 1)
            max_rows(0, 0)
            qk_hi(before, 0, 2)
            batch("first", 0)
            with act.Fori(1, B - 1) as b:
                batch("loop", b)
            batch("last", B - 1)
            o_hi_parts(("after", None))

        @block.vector
        def _(dve):
            links = [0]

            def link(instruction):
                links[0] += 1
                instruction.then_inc(chain, 1)
                dve.wait_ge(chain, links[0])

            def coefficients(n, tiles):
                for i in tiles:
                    st = dve.bn_stats(stats[:, i, :], X[:, i, :])
                st.then_inc(stats_done, 1)
                dve.wait_ge(stats_done, n + 1)
                for i in tiles:
                    mv = dve.bn_aggr(mean_var[:, i, :], stats[:, i, :])
                mv.then_inc(mv_done, 1)

            def first_coefficients():
                first = slice(0, TB)
                dve.wait_ge(mv_done, 1)
                link(dve.tensor_scalar(var_eps[:, first, :], mean_var[:, first, 1:2], EPS, None,
                                       ALU.add))
                dve.reciprocal(neg_mean[:, first, :], var_eps[:, first, :]).then_inc(ve_done, 1)
                dve.wait_ge(root_done, 1)
                refine_root(dve, link, rstd[:, first, :], var_eps[:, first, :],
                            neg_mean[:, first, :]).then_inc(rstd_done, 1)
                dve.wait_ge(rstd_done, 1)
                dve.scalar_tensor_tensor(out=neg_mean_rstd[:, first, :], in0=mean_var[:, first, 0:1],
                                         scalar=-1.0, in1=rstd[:, first, :], op0=ALU.mult,
                                         op1=ALU.mult).then_inc(coef_done, 1)

            def modulate(where, nb, uses):
                for c, use in enumerate(("xA", "xB", "xC")):
                    if use in uses:
                        k, n = ORDER.at(use, where)
                        dst = xt_rest[:, :] if c == 2 else xt[:, c, :]
                        rows = CR if c == 2 else P
                        dve.wait_ge(full[k], n)
                        dve.sem_inc(parted, 1)
                        dve.tensor_scalar(dst, ps_shared[0:rows, k, :],
                                          modT[0:rows, 1, c, bass.ds(nb, 1)],
                                          modT[0:rows, 0, c, bass.ds(nb, 1)],
                                          ALU.mult, ALU.add).then_inc(free[k], 1)

            def x_lo_rest(nb):
                dve.wait_ge(xs_hi, nb * 4 + 4)
                dve.tensor_tensor(XS[CR:2 * CR, 4, :], xt_rest[:, :], f(XS[0:CR, 4, :]),
                                  ALU.subtract).then_inc(xs_lo_rest, 1)

            def qkv(where, nb, i):
                (ka, na), (kb, nb_) = (ORDER.at(f"qkv{i}{h}", where) for h in "ab")
                bias = S["bqkv"]
                dst = (qk[:, i % 2, :].rearrange("p (g j d) -> p g j d", j=HG, d=HD) if head_norm
                       else QKN[:, i, :, :, :].rearrange("p g d j -> p g j d"))
                cut = HALF // GC
                if head_norm and (where[0] != "before" or i >= 2):
                    dve.wait_ge(cen_done, nb * TB + (i - 1))
                dve.wait_ge(full[ka], na)
                heads = lambda ap: ap.rearrange("p (g j d) -> p g j d", j=HG, d=HD)
                dve.tensor_tensor(dst[:, 0:cut], heads(ps_shared[:, ka, 0:HALF]),
                                  heads(bias[:, 0:HALF]), ALU.add).then_inc(free[ka], 1)
                dve.wait_ge(full[kb], nb_)
                rest = QKW - HALF
                dve.tensor_tensor(dst[:, cut:2 * NG], heads(ps_shared[:, kb, 0:rest]),
                                  heads(bias[:, HALF:QKW]), ALU.add).then_inc(qk_done if head_norm else qkn_done, 1)
                if where[0] != "before":
                    dve.wait_ge(v_done, nb)
                dve.tensor_tensor(v_in[:, i, :], ps_shared[:, kb, rest:HALF], bias[:, QKW:3 * C],
                                  ALU.add).then_inc(free[kb], 1)
                if head_norm:
                    n = nb * TB + (i + 1)
                    dve.wait_ge(qk_done, n)
                    dve.reduce_sum(h_sum[:, :], qk[:, i % 2, :].rearrange("p (h d) -> p h d", d=HD),
                                   AX).then_inc(h_sum_done, 1)
                    dve.wait_ge(h_sum_done, n)
                    dve.tensor_scalar(h_mean[:, i, :], h_sum[:, :], 1.0 / HD, None, ALU.mult
                                      ).then_inc(h_mean_done, 1)

            def head_squares(nb, i):
                dve.wait_ge(sq_done, nb * TB + (i + 1))
                dve.reduce_sum(h_var[:, i, :], qk_sq[:, :].rearrange("p (h d) -> p h d", d=HD),
                               AX).then_inc(h_var_done, 1)

            def first_reciprocals(i):
                dve.wait_ge(h_var_done, i + 1)
                link(dve.tensor_scalar(h_ve[:, :], h_var[:, i, :], 1.0 / HD, EPS, ALU.mult, ALU.add))
                dve.reciprocal(h_v[:, :], h_ve[:, :]).then_inc(h_v_done, 1)

            def first_roots(i):
                dve.wait_ge(root_done, i + 2)
                refine_root(dve, link, h_rstd[:, :], h_ve[:, :], h_v[:, :]).then_inc(h_rstd_done, 1)

            def head_gain(nb, i):
                dve.wait_ge(cen_scaled, nb * TB + (i + 1))
                for s_ in range(2):
                    half = QKN[:, i, NG * s_:NG * s_ + NG, :, :]
                    gn = dve.tensor_tensor(half, half,
                                           S["gain"][:, s_, :].unsqueeze(1).unsqueeze(3)
                                           .to_broadcast([P, NG, HD, HG]), ALU.mult)
                gn.then_inc(qkn_done, 1)

            def qk_lo(where, nb, g):
                for s_, name in enumerate("qk"):
                    k, _ = ORDER.at(f"{name}{g}", where)
                    dve.wait_ge(hi_done, nb * (2 * NG) + (2 * g + s_ + 1))
                    dve.tensor_tensor(src[:, LO_OF[name], :], ps_shared[0:GC, k, :],
                                      f(src[:, HI_OF[name], :]), ALU.subtract).then_inc(free[k], 1)

            def maxima(n, done):
                dve.wait_ge(max_full, done + (n + 1))
                dve.reduce_max(neg_max[:, (n % HG) * TB + n // HG:(n % HG) * TB + n // HG + 1],
                               ps_max[:, n % MAX_RING, :], AX, negate=True).then_inc(max_done, 1)

            def normalise_out(where, b, g):
                k, n = ORDER.at(f"o{g}", where)
                ps = ps_shared[:, k, :].rearrange("p (i j r) -> p i j r", i=TB, j=HG)
                dve.wait_ge(full[k], n)
                dve.reciprocal(rden[:, g, :, :].unsqueeze(3), ps[:, :, :, HD:HD + 1]).then_inc(rden_done, 1)
                dve.wait_ge(rden_done, b * NG + (g + 1))
                dve.tensor_tensor(ON[:, :, GC * g:GC * g + GC].rearrange("p i (j d) -> p i j d", j=HG),
                                  ps[:, :, :, 0:HD],
                                  rden[:, g, :, :].unsqueeze(3).to_broadcast([P, TB, HG, HD]),
                                  ALU.mult).then_inc(free[k], 1)

            def o_lo_parts(where, ob):
                for c, use in enumerate(("oA", "oB")):
                    k, _ = ORDER.at(use, where)
                    dve.wait_ge(o_hi, ob * 4 + (c + 1))
                    dve.tensor_tensor(XS[:, 2 + c, :], ps_shared[:, k, :], f(XS[:, c, :]),
                                      ALU.subtract).then_inc(free[k], 1)
                k, _ = ORDER.at("oC", where)
                dve.wait_ge(o_hi, ob * 4 + 4)
                dve.tensor_tensor(XS[CR:2 * CR, 4, :], ps_shared[0:CR, k, :], f(XS[0:CR, 4, :]),
                                  ALU.subtract).then_inc(free[k], 1)

            def projected(where, tiles):
                for i in tiles:
                    k, n = ORDER.at(f"proj{i}", where)
                    dve.wait_ge(full[k], n)
                    dve.tensor_tensor(y[:, i, :], ps_shared[:, k, 0:C], S["bproj"][:, :],
                                      ALU.add).then_inc(free[k], 1)

            def batch(section, b):
                where, nb = (section, b), b + 1
                prepares, projects = section != "last", section != "first"
                for g in range(NG):
                    for i in range(TB):
                        if g < NG - 1 or prepares:
                            for j in range(HG):
                                maxima(HG * i + j, b * (NG * SCORES) + SCORES * (g + 1))
                        if prepares and (g, i) == (0, 0):
                            modulate(where, nb, ("xA", "xB"))
                        if prepares and (g, i) == (0, 1):
                            modulate(where, nb, ("xC",))
                        if (g, i) == (0, 2):
                            if prepares:
                                x_lo_rest(nb)
                            qk_lo(where, b, NG - 1)
                        if prepares and (g, i) in ((0, 3), (1, 0), (1, 1)):
                            qkv(where, nb, {(0, 3): 0, (1, 0): 2, (1, 1): 3}[g, i])
                        if projects and (g, i) == (1, 2):
                            o_lo_parts(where, b - 1)
                        if (g, i) == (1, 3):
                            normalise_out(where, b, 0)
                        if prepares and head_norm:
                            if (g, i) == (1, 1):
                                head_squares(nb, 1)
                            if (g, i) == (1, 2):
                                head_gain(nb, 0)
                            if (g, i) == (1, 3):
                                head_squares(nb, 2)
                            if g == 2 and i < 3:
                                head_gain(nb, (1, 2, 3)[i])
                        if prepares and (g, i) == (2, QK0):
                            qk_lo(where, nb, 0)
                        if prepares and (g, i) == (3, 1):
                            qk_lo(where, nb, 1)
                    if g == 0:
                        if prepares:
                            qkv(where, nb, 1)
                            if head_norm:
                                head_squares(nb, 0)
                        continue
                    if prepares and head_norm and g == 1:
                        head_squares(nb, 3)
                    if projects and g < NG - 1:
                        if section == "last" and g == 1:
                            dve.wait_ge(x_done, B - 1)
                        projected(where, (2 * g - 2, 2 * g - 1))
                    if prepares and g == NG - 1:
                        qk_lo(where, nb, 2)
                    normalise_out(where, b, g)

            before, after = ("before", None), ("after", None)
            coefficients(0, range(TB))
            first_coefficients()
            dve.memset(ps_out[:, :], 0.0).then_inc(inited, 1)
            modulate(before, 0, ("xA", "xB", "xC"))
            x_lo_rest(0)
            coefficients(1, range(TB, T))
            if head_norm:
                qkv(before, 0, 0)
                qkv(before, 0, 1)
                head_squares(0, 0)
                first_reciprocals(0)
                qkv(before, 0, 2)
                first_roots(0)
                head_squares(0, 1)
                first_reciprocals(1)
                head_gain(0, 0)
                first_roots(1)
                qkv(before, 0, 3)
                head_gain(0, 1)
                head_squares(0, 2)
                first_reciprocals(2)
                first_roots(2)
                head_squares(0, 3)
                first_reciprocals(3)
                head_gain(0, 2)
                first_roots(3)
                head_gain(0, 3)
            else:
                for i in range(TB):
                    qkv(before, 0, i)
            qk_lo(before, 0, 0)
            qk_lo(before, 0, 1)
            for n in range(SCORES):
                maxima(n, 0)
            qk_lo(before, 0, 2)
            batch("first", 0)
            with dve.Fori(1, B - 1) as b:
                batch("loop", b)
            batch("last", B - 1)
            o_lo_parts(after, B - 1)
            dve.wait_ge(x_done, B)
            projected(after, range(TB))
            dve.wait_ge(late_in, LATE)
            for i in range(TB):
                k, n = ORDER.at(f"proj{i}", after)
                dve.wait_ge(free[k], n)
                dve.tensor_tensor(y[:, i, :], y[:, i, :], gates[:, 0, B - 1, :], ALU.mult
                                  ).then_inc(last_gated, 1)
            for i in range(TB):
                dve.wait_ge(last_gated, i + 1)
                x_tile = X[:, (B - 1) * TB + i, :]
                dve.tensor_tensor(x_tile, x_tile, y[:, i, :], ALU.add)

        @block.gpsimd
        def _(pool):
            def coefficients(n, tiles):
                pool.wait_ge(mv_done, n + 1)
                pool.tensor_scalar(var_eps[:, tiles, :], mean_var[:, tiles, 1:2], EPS, 1.0,
                                   ALU.add, ALU.mult)
                pool.tensor_scalar(neg_mean[:, tiles, :], mean_var[:, tiles, 0:1], -1.0, 1.0,
                                   ALU.mult, ALU.mult).then_inc(ve_done, 1)
                pool.wait_ge(ve_done, n + 1)
                pool.tensor_tensor(rstd[:, tiles, :], var_eps[:, tiles, :],
                                   S["neg_half"][:, tiles].unsqueeze(2), ALU.pow).then_inc(rstd_done, 1)
                pool.wait_ge(rstd_done, n + 1)
                pool.tensor_tensor(neg_mean_rstd[:, tiles, :], neg_mean[:, tiles, :], rstd[:, tiles, :],
                                   ALU.mult).then_inc(coef_done, 1)

            def x_lo(nb):
                for c in range(2):
                    pool.wait_ge(xs_hi, nb * 4 + (c + 1))
                    pool.tensor_tensor(XS[:, 2 + c, :], xt[:, c, :], f(XS[:, c, :]),
                                       ALU.subtract).then_inc(xs_lo, 1)

            def centre(where, nb, i):
                pool.wait_ge(h_mean_done, nb * TB + (i + 1))
                pool.tensor_tensor(
                    QKN[:, i, :, :, :].rearrange("p g d j -> p g j d"),
                    qk[:, i % 2, :].rearrange("p (g j d) -> p g j d", j=HG, d=HD),
                    h_mean[:, i, :].rearrange("p (g j) -> p g j", j=HG).unsqueeze(3)
                    .to_broadcast([P, 2 * NG, HG, HD]),
                    ALU.subtract).then_inc(cen_done, 1)

            def scale_heads(where, nb, i):
                n = nb * TB + (i + 1)
                if where[0] != "before":
                    pool.wait_ge(h_var_done, n)
                    pool.sem_inc(parted, 1)
                    pool.tensor_scalar(h_v[:, :], h_var[:, i, :], 1.0 / HD, EPS, ALU.mult, ALU.add
                                       ).then_inc(h_v_done, 1)
                    pool.wait_ge(h_v_done, n)
                    pool.tensor_tensor(h_rstd[:, :], h_v[:, :], S["neg_half"][:, :], ALU.pow
                                       ).then_inc(h_rstd_done, 1)
                pool.wait_ge(h_rstd_done, n)
                pool.tensor_tensor(
                    QKN[:, i, :, :, :].rearrange("p g d j -> p g j d"),
                    QKN[:, i, :, :, :].rearrange("p g d j -> p g j d"),
                    h_rstd[:, :].rearrange("p (g j) -> p g j", j=HG).unsqueeze(3)
                    .to_broadcast([P, 2 * NG, HG, HD]),
                    ALU.mult).then_inc(cen_scaled, 1)

            def copy_v(where, nb):
                k, n = ORDER.at("qkv3b", where)
                pool.wait_ge(free[k], n)
                if where[0] != "before":
                    pool.wait_ge(pv_done, nb * (NG * TB))
                    pool.sem_inc(parted, 1)
                pool.tensor_scalar(V[:, :, :, 0:HD].rearrange("p i h d -> p (i h) d"),
                                   v_in[:, :, :].rearrange("p i (h d) -> p (i h) d", d=HD),
                                   1.0, 1.0, ALU.mult, ALU.mult).then_inc(v_done, 1)

            def add_output(where, ob):
                for i in range(TB):
                    k, n = ORDER.at(f"proj{i}", where)
                    pool.wait_ge(free[k], n)
                pool.sem_inc(parted, 1)
                gate = gates[:, 0, bass.ds(ob, 1), :]
                pool.tensor_tensor(y[:, :, :], y[:, :, :], gate.to_broadcast([P, TB, C]), ALU.mult
                                   ).then_inc(y_gated, 1)
                pool.wait_ge(y_gated, ob + 1)
                pool.sem_inc(parted, 1)
                x_batch = X[:, bass.ds(ob * TB, TB), :]
                pool.tensor_tensor(x_batch, x_batch, y[:, :, :], ALU.add).then_inc(x_done, 1)

            def batch(section, b):
                where, nb = (section, b), b + 1
                if section != "last":
                    x_lo(nb)
                    if head_norm:
                        centre(where, nb, 0)
                        centre(where, nb, 1)
                        scale_heads(where, nb, 0)
                        centre(where, nb, 2)
                        centre(where, nb, 3)
                        for i in range(1, TB):
                            scale_heads(where, nb, i)
                if section != "first":
                    add_output(where, b - 1)
                if section != "last":
                    copy_v(where, nb)

            pool.memset(V[:, :, :, :], 1.0).then_inc(v_ones, 1)
            x_lo(0)
            if l > 0:
                clear_stacks(pool, S, rows_zero)
            coefficients(1, slice(TB, T))
            if head_norm:
                before = ("before", None)
                centre(before, 0, 0)
                centre(before, 0, 1)
                for i in range(TB):
                    scale_heads(before, 0, i)
                    if i + 2 < TB:
                        centre(before, 0, i + 2)
            pool.wait_ge(v_ones, 1)
            copy_v(("before", None), 0)
            pool.sem_inc(x_done, 1)
            batch("first", 0)
            pool.wait_ge(late_in, LATE)
            with pool.Fori(1, B - 1) as b:
                batch("loop", b)
            batch("last", B - 1)

        @block.sync
        def _(sp):
            def stacks(where, g):
                for name in "qk":
                    k, n = ORDER.at(f"{name}{g}", where)
                    sp.wait_ge(free[k], n)
                    sp.sem_inc(parted, 1)
                for at, parts in enumerate(PARTS):
                    for s_, part in enumerate(parts):
                        sp.dma_start(f(STK[g][HD * at:HD * at + HD, s_, :, :]), f(src[:, part, :])
                                     ).then_inc(loaded[g], 16)

            def max_row(g, n):
                sp.wait_ge(ring_done, n)
                sp.sem_inc(parted, 1)
                sp.dma_start(f(STK[g][M_ROW:M_ROW + 1, 0, :, :]), f(neg_max_rows[:, :])
                             ).then_inc(m_loaded, 16)

            def batch(section, b):
                where = (section, b)
                prepares = section != "last"
                stacks(where, NG - 1)
                for g in range(NG):
                    if g >= 2 and prepares:
                        stacks(where, g - 2)
                    if g < NG - 1 or prepares:
                        max_row((g + 1) % NG, events(b, g) + EVENTS)
                    if prepares:
                        sp.dma_start(f(STK[g][M_ROW:M_ROW + 1, 0, :, :]), f(zero_row[:, :])
                                     ).then_inc(loaded[g], 16)
                if prepares:
                    stacks(where, 2)

            for i, part in enumerate((2, 5)):
                sp.dma_start(gates[:, i, :, :],
                             S["mod_rows"][l][:, C * part:C * part + C].partition_broadcast(P)
                             ).then_inc(late_in, 16)
            for e in range(L["E"]):
                sp.dma_start(S["b2"][:, e, :], L["b2"][e, :].partition_broadcast(P)
                             ).then_inc(late_in, 16)
            if l > 0:
                sp.wait_ge(rows_zero, 2)
            stacks(("before", None), 0)
            if l > 0:
                sp.wait_ge(rows_zero, 1 + NG)
            stacks(("before", None), 1)
            max_row(0, 1)
            stacks(("before", None), 2)
            batch("first", 0)
            with sp.Fori(1, B - 1) as b:
                batch("loop", b)
            batch("last", B - 1)
            sp.wait_ge(late_in, LATE)


def mlp(nc, sem, sb, pb, L, S, following):
    l, E = L["l"], L["E"]
    X, ident, modT, gates = S["X"], S["ident"], S["modT"][l], S["gates"]
    RUNS = [(0, 4), (4, 8), (8, NHC)]
    NPIECES = 3 + len(RUNS)
    ctx = ExitStack()
    with ctx:
        def t(name, shape, dt=F32):
            return sb(ctx, f"{name}_m{l}", shape, dt)

        n_slots = 2 if E > 1 else 1
        stats = t("stats", [P, T, 6])
        mean_var = t("mean_var", [P, T, 2])
        var_eps = t("var_eps", [P, T, 1])
        neg_mean = t("neg_mean", [P, T, 1])
        rstd = t("rstd", [P, T, 1])
        neg_mean_rstd = t("neg_mean_rstd", [P, T, 1])
        xn = t("xn", [P, TB, C])
        xt = t("xt", [P, 2, NB])
        xt_rest = t("xt_rest", [CR, NB])
        XS = t("XS", [P, 5, B * NB], F32R)
        raw = t("raw", [P, 2, HID])
        W1 = [t(f"W1_{i}", [P, 5, HID], F32R) for i in range(n_slots)]
        W2 = [t(f"W2_{i}", [P, 2, NHC, C], F32R) for i in range(n_slots)]
        G = t("G", [P, 3, NB])
        HHI = t("HHI", [P, 3, NB], F32R)
        HLO = t("HLO", [P, 3, NB], F32R)
        y = t("y", [P, TB, C])
        logits = t("logits", [P, TB, 4])
        beats = t("beats", [P, 6, TB])
        rank = t("rank", [P, TB, 4])
        best = t("best", [P, TB])
        shifted = t("shifted", [P, TB, 4])
        ex = t("ex", [P, TB, 4])
        picked = t("picked", [P, TB, 4])
        total = t("total", [P, TB])
        rtotal = t("rtotal", [P, TB])
        cw = t("cw", [P, T, 4])

        ps_h = pb(ctx, f"ps_h{l}", [P, 3, 512], F32)
        ps_y = pb(ctx, f"ps_y{l}", [P, TB, 512], F32)
        ps_ln = pb(ctx, f"ps_ln{l}", [P, 512], F32)

        def s(name):
            return sem(f"{name}_m{l}")

        parted = s("parted")
        chain = s("chain")
        stats_done = s("stats_done")
        mv_done = s("mv_done")
        root_done = s("root_done")
        ve_done = s("ve_done")
        rstd_done = s("rstd_done")
        coef_done = s("coef_done")
        xn_done = s("xn_done")
        ln_full = s("ln_full")
        ln_free = s("ln_free")
        xs_hi = s("xs_hi")
        xs_lo = s("xs_lo")
        xs_lo_rest = s("xs_lo_rest")
        shifted_done = s("shifted_done")
        ex_done = s("ex_done")
        cw_done = s("cw_done")
        first_in = [s(f"first_in{n}") for n in range(6)]
        raw_in = [s("raw_in0"), s("raw_in1")]
        hi_split = s("hi_split")
        split_done = s("split_done")
        h_full = s("h_full")
        gelu_done = s("gelu_done")
        h_hi = s("h_hi")
        h_lo = s("h_lo")
        h_used = s("h_used")
        y_full = s("y_full")
        y_free = s("y_free")
        y_gated = s("y_gated")
        x_done = s("x_done")
        out_done = s("out_done")

        LN_USES = 4 if E > 1 else 3
        PIECE_DMAS = [1, 1, 3, 1, 1, 1]

        ahead = AttentionWeights(ctx, sem, sb, following, S) if following else None

        def arrived(e, n):
            slot = n % 2
            before = sum(PIECE_DMAS[m] for m in range(NPIECES) if m % 2 == slot) * (e - 1)
            return slot, 16 * (before + sum(PIECE_DMAS[m] for m in range(n + 1) if m % 2 == slot))

        def raw_piece(e, n):
            if (e, n) == (0, 2):
                return y[:, :, :].rearrange("p t c -> p (t c)")
            if (e, n) == (0, 3):
                return G[:, :, :].rearrange("p s n -> p (s n)")[:, 0:HID]
            return raw[:, n % 2, :]

        block = ctx.enter_context(nc.Block())

        @block.sync
        def _(sp):
            for e in range(E):
                w1, w2 = L["w1"][e], L["w2"][e]
                for n in range(NPIECES):
                    if e >= 1:
                        sp.wait_ge(split_done, e * NPIECES + n - 1)
                    elif n >= 4:
                        sp.wait_ge(split_done, n - 3)
                    stage = raw_piece(e, n)
                    there = first_in[n] if e == 0 else raw_in[n % 2]
                    if n < 2:
                        sp.dma_start(stage, w1[P * n:P * n + P, :]).then_inc(there, 16)
                    elif n == 2:
                        for r in range(3):
                            sp.dma_start(stage[CR * r:CR * r + CR, :], w1[2 * P:C, :]
                                         ).then_inc(there, 16)
                    else:
                        a, z = RUNS[n - 3]
                        sp.dma_start(stage[:, 0:C * (z - a)].rearrange("p (k n) -> p k n", n=C),
                                     w2[P * a:P * z, :].rearrange("(k p) n -> p k n", p=P)
                                     ).then_inc(there, 16)
            if ahead:
                ahead.load(sp)
                ahead.wait_biases(sp)
            if L["out"] is not None:
                for b in range(B):
                    sp.wait_ge(x_done, ((E - 1) * B + b + 1) * TB)
                    sp.dma_start(L["out"][b].rearrange("(t p) c -> p t c", p=P),
                                 X[:, TB * b:TB * b + TB, :]).then_inc(out_done, 16)
                sp.wait_ge(out_done, 16 * B)

        def piece(e, n):
            k, stage = e % n_slots, raw_piece(e, n)
            if n < 2:
                hi = W1[k][:, n, :]
                return stage, hi, stage, hi, W1[k][:, 2 + n, :]
            if n == 2:
                lo = W1[k][2 * CR:3 * CR, 4, :]
                return stage[0:3 * CR, :], W1[k][0:3 * CR, 4, :], stage[2 * CR:3 * CR, :], lo, lo
            a, z = RUNS[n - 3]
            src = stage[:, 0:C * (z - a)].rearrange("p (k n) -> p k n", n=C)
            hi = W2[k][:, 0, a:z, :]
            return src, hi, src, hi, W2[k][:, 1, a:z, :]

        @block.gpsimd
        def _(pool):
            def coefficients(n, tiles):
                pool.wait_ge(mv_done, n + 1)
                pool.tensor_scalar(var_eps[:, tiles, :], mean_var[:, tiles, 1:2], EPS, 1.0,
                                   ALU.add, ALU.mult)
                pool.tensor_scalar(neg_mean[:, tiles, :], mean_var[:, tiles, 0:1], -1.0, 1.0,
                                   ALU.mult, ALU.mult).then_inc(ve_done, 1)
                pool.wait_ge(ve_done, n + 1)
                pool.tensor_tensor(rstd[:, tiles, :], var_eps[:, tiles, :],
                                   S["neg_half"][:, tiles].unsqueeze(2), ALU.pow).then_inc(rstd_done, 1)
                pool.wait_ge(rstd_done, n + 1)
                pool.tensor_tensor(neg_mean_rstd[:, tiles, :], neg_mean[:, tiles, :], rstd[:, tiles, :],
                                   ALU.mult).then_inc(coef_done, 1)

            def split_piece(e, n):
                m = e * NPIECES + n
                slot, there = arrived(e, n)
                src, hi, lo_src, lo_hi, lo = piece(e, n)
                pool.wait_ge(raw_in[slot], there)
                pool.wait_ge(split_done, m)
                pool.tensor_scalar(hi, src, 1.0, 1.0, ALU.mult, ALU.mult).then_inc(hi_split, 1)
                pool.wait_ge(hi_split, m + 1)
                pool.tensor_tensor(lo, lo_src, f(lo_hi), ALU.subtract).then_inc(split_done, 1)

            def x_lo(b):
                for c in range(2):
                    pool.wait_ge(xs_hi, 4 * b + c + 1)
                    pool.tensor_tensor(XS[:, 2 + c, NB * b:NB * b + NB], xt[:, c, :],
                                       f(XS[:, c, NB * b:NB * b + NB]), ALU.subtract).then_inc(xs_lo, 1)

            x_lo(0)
            coefficients(1, slice(TB, T))
            if ahead:
                pool.wait_ge(xs_lo, 2)
                ahead.split(pool, lambda hi, src: pool.tensor_scalar(hi, src, 1.0, 1.0, ALU.mult, ALU.mult))
            for b in range(1, B):
                x_lo(b)
            for e in range(1, E):
                if e >= 2:
                    pool.wait_ge(y_full, (e - 1) * B * TB)
                for n in range(NPIECES):
                    split_piece(e, n)

        @block.scalar
        def _(act):
            def normalise(b):
                act.wait_ge(coef_done, min(b, 1) + 1)
                if b >= 1:
                    act.wait_ge(ln_full, LN_USES * (b - 1) + 3)
                for i in range(TB * b, TB * b + TB):
                    act.activation(xn[:, i % TB, :], X[:, i, :], ACT.Identity,
                                   bias=neg_mean_rstd[:, i, :], scale=rstd[:, i, :]).then_inc(xn_done, 1)

            def x_hi(b, c):
                cols = slice(NB * b, NB * b + NB)
                act.wait_ge(ln_free, LN_USES * b + c + 1)
                if c < 2:
                    act.activation(XS[:, c, cols], xt[:, c, :], ACT.Copy).then_inc(xs_hi, 1)
                else:
                    for at in (0, 2 * CR):
                        act.activation(XS[at:at + CR, 4, cols], xt_rest[:, :], ACT.Copy
                                       ).then_inc(xs_hi, 1)

            def piece_hi(n):
                act.wait_ge(first_in[n], 16 * PIECE_DMAS[n])
                act.activation(piece(0, n)[1], piece(0, n)[0], ACT.Copy).then_inc(hi_split, 1)

            def weights_exp(b):
                if E > 1:
                    act.wait_ge(shifted_done, b + 1)
                    act.activation(ex[:, :, :], shifted[:, :, :], ACT.Exp).then_inc(ex_done, 1)

            def gelu(i, e, c):
                n = i * NHC + c
                act.wait_ge(h_full, n + 1)
                if not isinstance(n, int) or n >= 3:
                    act.wait_ge(h_lo, n - 2)
                act.activation(G[:, c % 3, :], ps_h[:, c % 3, :], ACT.Gelu_apprx_tanh,
                               bias=S["b1T"][l][:, NHC * e + c:NHC * e + c + 1]).then_inc(gelu_done, 1)

            act.wait_ge(ve_done, 1)
            act.activation(rstd[:, 0:TB, :], neg_mean[:, 0:TB, :], ACT.Sqrt).then_inc(root_done, 1)
            normalise(0)
            piece_hi(0)
            piece_hi(1)
            for c in range(3):
                x_hi(0, c)
            for n in range(2, NPIECES):
                piece_hi(n)
            act.wait_ge(split_done, 4)
            for b in range(B):
                for c in range(NHC):
                    gelu(b, 0, c)
                    if c == 1:
                        weights_exp(b)
                        if b + 1 < B:
                            normalise(b + 1)
                    if c in (4, 5, 6) and b + 1 < B:
                        x_hi(b + 1, c - 4)
            for e in range(1, E):
                with act.Fori(0, B) as b:
                    for c in range(NHC):
                        gelu(e * B + b, e, c)

        @block.vector
        def _(dve):
            links = [0]

            def link(instruction):
                links[0] += 1
                instruction.then_inc(chain, 1)
                dve.wait_ge(chain, links[0])

            def coefficients(n, tiles):
                for i in tiles:
                    st = dve.bn_stats(stats[:, i, :], X[:, i, :])
                st.then_inc(stats_done, 1)
                dve.wait_ge(stats_done, n + 1)
                for i in tiles:
                    mv = dve.bn_aggr(mean_var[:, i, :], stats[:, i, :])
                mv.then_inc(mv_done, 1)

            def first_coefficients():
                first = slice(0, TB)
                dve.wait_ge(mv_done, 1)
                link(dve.tensor_scalar(var_eps[:, first, :], mean_var[:, first, 1:2], EPS, None,
                                       ALU.add))
                dve.reciprocal(neg_mean[:, first, :], var_eps[:, first, :]).then_inc(ve_done, 1)
                dve.wait_ge(root_done, 1)
                refine_root(dve, link, rstd[:, first, :], var_eps[:, first, :],
                            neg_mean[:, first, :]).then_inc(rstd_done, 1)
                dve.wait_ge(rstd_done, 1)
                dve.scalar_tensor_tensor(out=neg_mean_rstd[:, first, :], in0=mean_var[:, first, 0:1],
                                         scalar=-1.0, in1=rstd[:, first, :], op0=ALU.mult,
                                         op1=ALU.mult).then_inc(coef_done, 1)

            def piece_lo(n):
                _, _, src, hi, lo = piece(0, n)
                dve.wait_ge(hi_split, n + 1)
                dve.tensor_tensor(lo, src, f(hi), ALU.subtract).then_inc(split_done, 1)

            def modulate(b, c):
                if b >= 1 and c == 0:
                    dve.wait_ge(xs_lo, 2 * b)
                    dve.wait_ge(xs_hi, 4 * b)
                    dve.wait_ge(xs_lo_rest, b)
                rows = (P, P, CR)[c]
                dst = xt_rest[:, :] if c == 2 else xt[:, c, :]
                dve.wait_ge(ln_full, LN_USES * b + c + 1)
                dve.tensor_scalar(dst, ps_ln[0:rows, :], modT[0:rows, 3, c, b:b + 1],
                                  modT[0:rows, 2, c, b:b + 1], ALU.mult, ALU.add
                                  ).then_inc(ln_free, 1)

            def x_lo_rest(b):
                dve.wait_ge(xs_hi, 4 * b + 4)
                cols = slice(NB * b, NB * b + NB)
                dve.tensor_tensor(XS[CR:2 * CR, 4, cols], xt_rest[:, :], f(XS[0:CR, 4, cols]),
                                  ALU.subtract).then_inc(xs_lo_rest, 1)

            def rank_experts(b):
                dve.wait_ge(ln_full, LN_USES * b + 4)
                dve.tensor_copy(logits[:, :, :], ps_ln[:, 0:4 * TB].rearrange("p (t e) -> p t e", e=4)
                                ).then_inc(ln_free, 1)
                dve.wait_ge(ln_free, LN_USES * b + 4)
                pairs = [(lo, hi) for hi in range(4) for lo in range(hi)]
                for n, (lo, hi) in enumerate(pairs):
                    dve.tensor_tensor(beats[:, n, :], logits[:, :, lo], logits[:, :, hi], ALU.is_ge)
                link(dve.reduce_max(best[:, :], logits[:, :, :], AX))
                for e in range(4):
                    start = float(sum(lo == e for lo, _ in pairs))
                    n, (lo, hi) = next((n, p) for n, p in enumerate(pairs) if e in p)
                    sign = -1.0 if lo == e else 1.0
                    step = dve.tensor_scalar(rank[:, :, e], beats[:, n, :], sign, start, ALU.mult, ALU.add)
                link(step)
                for turn in (1, 2):
                    for e in range(4):
                        n, (lo, hi) = [(n, p) for n, p in enumerate(pairs) if e in p][turn]
                        step = dve.tensor_tensor(rank[:, :, e], rank[:, :, e], beats[:, n, :],
                                                 ALU.subtract if lo == e else ALU.add)
                    link(step)
                dve.tensor_tensor(shifted[:, :, :], logits[:, :, :],
                                  best[:, :].unsqueeze(2).to_broadcast([P, TB, 4]), ALU.subtract
                                  ).then_inc(shifted_done, 1)

            def weigh_experts(b):
                dve.wait_ge(ex_done, b + 1)
                link(dve.scalar_tensor_tensor(out=picked[:, :, :], in0=rank[:, :, :], scalar=2.0,
                                              in1=ex[:, :, :], op0=ALU.is_lt, op1=ALU.mult))
                link(dve.reduce_sum(total[:, :], picked[:, :, :], AX))
                link(dve.reciprocal(rtotal[:, :], total[:, :]))
                dve.tensor_tensor(cw[:, TB * b:TB * b + TB, :], picked[:, :, :],
                                  rtotal[:, :].unsqueeze(2).to_broadcast([P, TB, 4]), ALU.mult
                                  ).then_inc(cw_done, 1)
                dve.wait_ge(cw_done, b + 1)

            def split_h(i, c):
                n = i * NHC + c
                dve.wait_ge(gelu_done, n + 1)
                if not isinstance(i, int) or i >= 1 or c >= 3:
                    if c >= 3:
                        dve.wait_ge(h_used, i * 8 + (c - 2))
                    elif c == 2:
                        dve.wait_ge(y_full, i * TB)
                    else:
                        dve.wait_ge(h_used, i * 8 - (1 - c))
                dve.tensor_copy(HHI[:, c % 3, :], G[:, c % 3, :]).then_inc(h_hi, 1)
                dve.wait_ge(h_hi, n + 1)
                dve.tensor_tensor(HLO[:, c % 3, :], G[:, c % 3, :], f(HHI[:, c % 3, :]),
                                  ALU.subtract).then_inc(h_lo, 1)

            def accumulate(i, e, b):
                for k in range(TB):
                    dve.wait_ge(y_full, i * TB + (k + 1))
                    dve.tensor_tensor(y[:, k, :], ps_y[:, k, 0:C], S["b2"][:, e, :], ALU.add
                                      ).then_inc(y_free, 1)
                for k in range(TB):
                    dve.wait_ge(y_free, i * TB + (k + 1))
                    dve.sem_inc(parted, 1)
                    dve.tensor_tensor(y[:, k:k + 1, :], y[:, k:k + 1, :], gates[:, 1, bass.ds(b, 1), :],
                                      ALU.mult).then_inc(y_gated, 1)
                for k in range(TB):
                    dve.wait_ge(y_gated, i * TB + (k + 1))
                    dve.sem_inc(parted, 1)
                    x_tile = X[:, bass.ds(b * TB + k, 1), :]
                    if E > 1:
                        dve.scalar_tensor_tensor(out=x_tile, in0=y[:, k:k + 1, :],
                                                 scalar=cw[:, bass.ds(b * TB + k, 1), e:e + 1],
                                                 in1=x_tile, op0=ALU.mult, op1=ALU.add
                                                 ).then_inc(x_done, 1)
                    else:
                        dve.tensor_tensor(x_tile, x_tile, y[:, k:k + 1, :], ALU.add).then_inc(x_done, 1)

            coefficients(0, range(TB))
            first_coefficients()
            piece_lo(0)
            for c in range(3):
                modulate(0, c)
            piece_lo(1)
            x_lo_rest(0)
            piece_lo(2)
            coefficients(1, range(TB, T))
            for n in range(3, NPIECES):
                piece_lo(n)
            for b in range(B):
                for c in range(NHC):
                    split_h(b, c)
                    if E > 1 and c == 0:
                        rank_experts(b)
                    if E > 1 and c == 2:
                        weigh_experts(b)
                    if c in (3, 4, 5) and b + 1 < B:
                        modulate(b + 1, c - 3)
                    if c == 7 and b + 1 < B:
                        x_lo_rest(b + 1)
                accumulate(b, 0, b)
            for e in range(1, E):
                with dve.Fori(0, B) as b:
                    for c in range(NHC):
                        split_h(e * B + b, c)
                    accumulate(e * B + b, e, b)

        @block.tensor
        def _(pe):
            def x_transposes(b, c):
                n, rows = LN_USES * b + c, (P, P, CR)[c]
                pe.wait_ge(xn_done, TB * b + TB)
                if n >= 1:
                    pe.wait_ge(ln_free, n)
                for i in range(TB):
                    mm = pe.transpose(ps_ln[0:rows, P * i:P * i + P],
                                      xn[:, i, P * c:P * c + rows], ident[:, :])
                mm.then_inc(ln_full, 1)

            def stack_ready(b):
                pe.wait_ge(xs_hi, 4 * b + 4)
                pe.wait_ge(xs_lo, 2 * b + 2)
                pe.wait_ge(xs_lo_rest, b + 1)

            def route_logits(b):
                if E > 1:
                    pe.wait_ge(ln_free, LN_USES * b + 3)
                    for i in range(TB):
                        at = P * (TB * b + i)
                        for n, (w, x) in enumerate(PAIRS):
                            r = rows_of(w)
                            mm = pe.matmul(ps_ln[:, 4 * i:4 * i + 4], XS[0:r, x, at:at + P],
                                           S["Wgate"][0:r, w, :], start=(n == 0),
                                           stop=(n == len(PAIRS) - 1))
                    mm.then_inc(ln_full, 1)

            def up(i, e, b, c):
                n = i * NHC + c
                if not isinstance(n, int) or n >= 3:
                    pe.wait_ge(gelu_done, n - 2)
                for m, (w, x) in enumerate(PAIRS):
                    r = rows_of(w)
                    mm = pe.matmul(ps_h[:, c % 3, :], W1[e % n_slots][0:r, w, P * c:P * c + P],
                                   XS[0:r, x, bass.ds(b * NB, NB)], start=(m == 0),
                                   stop=(m == len(PAIRS) - 1))
                mm.then_inc(h_full, 1)

            def down(i, e, c):
                if c == 0 and (not isinstance(i, int) or i >= 1):
                    pe.wait_ge(y_free, i * TB)
                pe.wait_ge(h_lo, i * NHC + (c + 1))
                if isinstance(i, int) and i == 0:
                    pe.wait_ge(split_done, 4 + sum(c >= z for _, z in RUNS))
                w2 = W2[e % n_slots]
                for k in range(TB):
                    cols = slice(P * k, P * k + P)
                    for m, (h, w) in enumerate(((HHI, 0), (HHI, 1), (HLO, 0))):
                        mm = pe.matmul(ps_y[:, k, 0:C], h[:, c % 3, cols], w2[:, w, c, :],
                                       start=(c == 0 and m == 0), stop=(c == NHC - 1 and m == 2))
                    if c == NHC - 1:
                        mm.then_inc(y_full, 1)
                if c < NHC - 1:
                    mm.then_inc(h_used, 1)

            def expert(i, e, b, between=None):
                for c in range(NHC):
                    up(i, e, b, c)
                    if c >= 2:
                        down(i, e, c - 2)
                    if between is not None:
                        between(b + 1, c)
                down(i, e, NHC - 2)
                down(i, e, NHC - 1)

            def prepare(b, c):
                if c in (3, 4, 5):
                    x_transposes(b, c - 3)
                if c == NHC - 1:
                    stack_ready(b)
                    route_logits(b)

            for c in range(3):
                x_transposes(0, c)
            stack_ready(0)
            route_logits(0)
            pe.wait_ge(split_done, 3)
            for b in range(B):
                expert(b, 0, b, prepare if b + 1 < B else None)
            for e in range(1, E):
                pe.wait_ge(split_done, (e + 1) * NPIECES)
                with pe.Fori(0, B) as b:
                    expert(e * B + b, e, b)


def build(nc, A, out):
    outer = ExitStack()
    with outer:
        layer_sems = []

        def sem(name):
            layer_sems.append(nc.alloc_semaphore(name=name))
            return layer_sems[-1]

        def sb(ctx, name, shape, dt):
            return ctx.enter_context(nc.sbuf_tensor(name, shape, dt))

        def pb(ctx, name, shape, dt):
            return ctx.enter_context(nc.psum_tensor(name, shape, dt))

        S = {name: sb(outer, name, shape, dt) for name, shape, dt in (
            ("X", [P, T, C], F32),
            ("ident", [P, P], F32),
            ("neg_half", [P, 2 * NH], F32),
            ("gates", [P, 2, B, C], F32),
            ("b2", [P, 4, C], F32),
            ("Wgate", [P, 5, 4], F32R),
        )}
        S["modT"] = [sb(outer, f"modT{l}", [P, 4, 3, B], F32) for l in range(2)]
        S["b1T"] = [sb(outer, f"b1T{l}", [P, 4 * NHC], F32) for l in range(2)]
        S["mod_rows"] = nc.dram_tensor("mod_rows", (2, B, 6 * C), F32, kind="Internal").ap()
        layers = []
        for l, p in enumerate(("L0_cond_", "L1_cond_")):
            one = l == 0
            L = {"l": l, "E": 1 if one else 4, "x": A["x"], "cond": A["cond_1152"],
                 "out": None if one else out}
            for name in ("w_qkv", "b_qkv", "w_proj", "b_proj"):
                L[name] = A[p + name]
            L["w_mod"], L["b_mod"] = ((A[p + "w_mod"], A[p + "b_mod"]) if one
                                      else (A[p + "w_adaln"], A[p + "b_adaln"]))
            if one:
                L["g_q"], L["g_k"] = A[p + "g_q"], A[p + "g_k"]
                for name in ("w1", "w2", "b1", "b2"):
                    L[name] = A[p + name].unsqueeze(0)
            else:
                for name in ("w1", "w2", "b1", "b2", "w_gate"):
                    L[name] = A[p + name]
            layers.append(L)

        def attention_weights(ctx, l):
            for name, shape, dt in (("Wqkv", [P, 5, 3 * C], F32R), ("Wproj", [P, 5, C], F32R),
                                    ("bqkv", [P, 3 * C], F32), ("bproj", [P, C], F32),
                                    ("gain", [P, 2, HD], F32)):
                S[name] = sb(ctx, f"{name}{l}", shape, dt)

        def attention_stacks(ctx, l):
            S["zero_row"] = sb(ctx, f"zero_row{l}", [NH, P], F32R)
            for g in range(NG):
                S[f"STK{g}"] = sb(ctx, f"STK{g}_{l}", [KS_ROWS, 2, HG, NB], F32R)

        with ExitStack() as first:
            attention_weights(first, 0)
            attention_stacks(first, 0)
            setup(nc, sem, sb, pb, layers, S)
            attention(nc, sem, sb, pb, layers[0], S)
        with ExitStack() as second:
            attention_weights(second, 1)
            mlp(nc, sem, sb, pb, layers[0], S, layers[1])
            nc.clear_and_free_semaphores(layer_sems)
            nc.all_engine_barrier()
            layer_sems = []
            attention_stacks(second, 1)
            attention(nc, sem, sb, pb, layers[1], S)
        mlp(nc, sem, sb, pb, layers[1], S, None)


_INS = ['x', 'cond_1152', 'L0_cond_w_mod', 'L0_cond_b_mod', 'L0_cond_w_qkv', 'L0_cond_b_qkv',
        'L0_cond_g_q', 'L0_cond_g_k', 'L0_cond_w_proj', 'L0_cond_b_proj', 'L0_cond_w1', 'L0_cond_b1',
        'L0_cond_w2', 'L0_cond_b2', 'L1_cond_w_adaln', 'L1_cond_b_adaln', 'L1_cond_w_qkv',
        'L1_cond_b_qkv', 'L1_cond_w_proj', 'L1_cond_b_proj', 'L1_cond_w_gate', 'L1_cond_w1',
        'L1_cond_b1', 'L1_cond_w2', 'L1_cond_b2']


def kernel(**inputs):
    import numpy as _np
    import concourse.bacc as _bacc
    from concourse import mybir as _mybir
    from concourse.bass_utils import run_bass_kernel_spmd as _run

    nc = _bacc.Bacc("TRN2", target_bir_lowering=False, num_devices=1)
    arrays, args = {}, {}
    for name in _INS:
        a = _np.ascontiguousarray(inputs[name])
        arrays[f"in_{name}"] = a
        args[name] = nc.dram_tensor(f"in_{name}", a.shape, _mybir.dt.from_np(a.dtype),
                                    kind="ExternalInput").ap()
    out = nc.dram_tensor("out_0", (B, NB, C), F32, kind="ExternalOutput").ap()
    build(nc, args, out)
    r = _run(nc, [arrays], core_ids=[0])
    return r.results[0]["out_0"]
```
